# Optimizing a Trainium2 kernel written in Bass

```python
import numpy as np
import jax
import jax.numpy as jnp

def _softmax(x, axis=-1):
    return jax.nn.softmax(x, axis=axis)

def _gelu(x):
    return jax.nn.gelu(x, approximate=True)

def _silu(x):
    return jax.nn.silu(x)

def _sigmoid(x):
    return jax.nn.sigmoid(x)

def _layernorm(x, axis=-1, eps=1e-05):
    m = jnp.mean(x, axis=axis, keepdims=True)
    v = jnp.var(x, axis=axis, keepdims=True)
    return (x - m) / jnp.sqrt(v + eps)

def _scatter_add(tgt, idx, src, axis=0):
    return tgt.at[idx].add(src)

def _segment_sum(src, seg, n):
    return jax.ops.segment_sum(src, seg, n)
kernel_name = 'mk_cond_resid_d2_seqx_r2_108ed7'

def setup_inputs(seed: int=0):
    np.random.seed(seed)
    _w = jnp.asarray

    def _rec_inputs():
        import jax
        import jax.numpy as jnp
        _rk = jax.random.key(seed)
        x = -7.109e-05 + 0.9999 * jax.random.normal(jax.random.fold_in(_rk, 1), (8, 512, 2048), jnp.float32)
        _lenS = 512 - jax.random.randint(jax.random.fold_in(_rk, 7), (8,), 0, max(1, 512 // 4) + 1, jnp.int32)
        _lenS2 = 512 - jax.random.randint(jax.random.fold_in(_rk, 8), (8,), 0, max(1, 512 // 4) + 1, jnp.int32)
        itok_B_4_50 = jax.random.randint(jax.random.fold_in(_rk, 11), (8,), 4, 51, jnp.int32)
        condB_scale = 0.000342416 + 0.0128191 * jax.random.normal(jax.random.fold_in(_rk, 12), (8,), jnp.float32)
        itok_Bx4096x4096_0_255 = jax.random.randint(jax.random.fold_in(_rk, 13), (8, 2048, 2048), 0, 128, jnp.int32)
        condB_wscale = jax.random.uniform(jax.random.fold_in(_rk, 14), (8,), jnp.float32, 0.0, 0.00091742)
        itok_Bx4096_0_255 = jax.random.randint(jax.random.fold_in(_rk, 16), (8, 2048), 0, 128, jnp.int32)
        condB_bscale = jax.random.uniform(jax.random.fold_in(_rk, 17), (8,), jnp.float32, 0.0, 0.000800939)
        return (x, itok_B_4_50, condB_scale, itok_Bx4096x4096_0_255, condB_wscale, itok_Bx4096_0_255, condB_bscale, _lenS)
    x, itok_B_4_50, condB_scale, itok_Bx4096x4096_0_255, condB_wscale, itok_Bx4096_0_255, condB_bscale, _lenS = _rec_inputs()

    def _L0_cond_setup():
        import jax, jax.numpy as jnp
        import numpy as np
        RANK = 16
        ALPHA = 16.0
        SCALING = ALPHA / RANK
        key = jax.random.key(seed)
        k1, k2, k3, k4 = jax.random.split(key, 4)
        batch, n_tok, d_in, d_out, n_adapters, rank = (8, 1024, 2048, 2048, 64, RANK)
        x = jax.random.normal(k1, (batch, n_tok, d_in), dtype=jnp.float32)
        A = jax.random.normal(k2, (n_adapters, d_out, rank), dtype=jnp.float32) * 0.02
        B = jax.random.normal(k3, (n_adapters, rank, d_in), dtype=jnp.float32)
        adapter_ids = jax.random.randint(k4, (batch,), 0, n_adapters, dtype=jnp.int32)
        return {'x': x, 'A': A, 'B': B, 'adapter_ids': adapter_ids}
    _L0_cond_all = _L0_cond_setup()
    _L0_cond_in = {k: v for k, v in _L0_cond_all.items() if k in ('A', 'B')}
    del _L0_cond_all

    def _L1_cond_setup():
        import jax, jax.numpy as jnp
        import numpy as np
        key = jax.random.key(seed)
        ks = jax.random.split(key, 10)
        N, OUT, IN = (8, 2048, 2048)
        B, S = (8, 1024)
        return {'x': jax.random.normal(ks[0], (B, S, IN), dtype=jnp.float32), 'weight': jax.random.normal(ks[1], (OUT, IN), dtype=jnp.float32) * 0.02, 'bias': jax.random.normal(ks[2], (OUT,), dtype=jnp.float32) * 0.02, 'scale': jax.random.normal(ks[3], (N,), dtype=jnp.float32) * 0.01, 'wq': jax.random.randint(ks[4], (N, OUT, IN), 0, 128, dtype=jnp.int32), 'wscale': jax.random.uniform(ks[5], (N,), dtype=jnp.float32) * 0.001, 'wzp': jax.random.randint(ks[6], (N,), 0, 128, dtype=jnp.int32), 'bq': jax.random.randint(ks[7], (N, OUT), 0, 128, dtype=jnp.int32), 'bscale': jax.random.uniform(ks[8], (N,), dtype=jnp.float32) * 0.001, 'bzp': jax.random.randint(ks[9], (N,), 0, 128, dtype=jnp.int32)}
    _L1_cond_all = _L1_cond_setup()
    _L1_cond_in = {k: v for k, v in _L1_cond_all.items() if k in ('weight', 'bias')}
    del _L1_cond_all
    return {'x': x, 'itok_B_4_50': itok_B_4_50, 'condB_scale': condB_scale, 'itok_Bx4096x4096_0_255': itok_Bx4096x4096_0_255, 'condB_wscale': condB_wscale, 'itok_Bx4096_0_255': itok_Bx4096_0_255, 'condB_bscale': condB_bscale, '_lenS': _lenS, 'L0_cond_A': _L0_cond_in['A'], 'L0_cond_B': _L0_cond_in['B'], 'L1_cond_weight': _L1_cond_in['weight'], 'L1_cond_bias': _L1_cond_in['bias']}

def reference(x, itok_B_4_50, condB_scale, itok_Bx4096x4096_0_255, condB_wscale, itok_Bx4096_0_255, condB_bscale, _lenS, L0_cond_A, L0_cond_B, L1_cond_weight, L1_cond_bias):
    import jax
    import jax.numpy as jnp

    def _L0_cond_ref(x, A, B, adapter_ids):
        import jax, jax.numpy as jnp
        import numpy as np
        RANK = 16
        ALPHA = 16.0
        SCALING = ALPHA / RANK
        B_req = B[adapter_ids]
        A_req = A[adapter_ids]
        Bx = jnp.einsum('bni,bri->bnr', x, B_req)
        out = jnp.einsum('bnr,bor->bno', Bx, A_req)
        return out * SCALING

    def _L1_cond_ref(x, weight, bias, scale, wq, wscale, wzp, bq, bscale, bzp):
        import jax, jax.numpy as jnp
        import numpy as np
        f32 = jnp.float32
        dW = jnp.einsum('i,ijk->jk', scale * wscale, wq.astype(f32)) + jnp.dot(scale, wzp.astype(f32))
        W = weight + dW
        db = jnp.einsum('i,ij->j', scale * bscale, bq.astype(f32)) + jnp.dot(scale, bzp.astype(f32))
        b = bias + db
        return jnp.einsum('bsi,oi->bso', x, W) + b
    x = x + _L0_cond_ref(x, L0_cond_A, L0_cond_B, itok_B_4_50)
    x = x + _L1_cond_ref(x, L1_cond_weight, L1_cond_bias, condB_scale, itok_Bx4096x4096_0_255, condB_wscale, _lenS, itok_Bx4096_0_255, condB_bscale, _lenS)
    return x

_drawn_inputs = setup_inputs


def setup_inputs(seed=0):
    import zlib

    import numpy as np

    out = dict(_drawn_inputs(seed))
    spreads = {}
    factors = {'condB_wscale': 64.0, 'condB_bscale': 200.0, 'L1_cond_bias': 200.0}
    for name, (base, spread) in spreads.items():
        noise = np.random.default_rng([zlib.crc32(name.encode()), seed]).standard_normal(out[name].shape)
        drawn = base * np.exp(spread * noise) if base else spread * noise
        out[name] = jnp.asarray(drawn.astype(out[name].dtype))
    for name, factor in factors.items():
        out[name] = (out[name] * factor).astype(out[name].dtype)
    return out
```

```python
def build_program(nc, x, ids, scale, wq, wscale, bq, bscale, zp, lora_a, lora_b, weight, bias, out):
    import concourse.bass as bass
    from concourse import mybir
    from contextlib import ExitStack

    F32, F32R, F16 = mybir.dt.float32, mybir.dt.float32r, mybir.dt.float16
    BF16, I32 = mybir.dt.bfloat16, mybir.dt.int32
    ALU, ACT, AX = mybir.AluOpType, mybir.ActivationFunctionType, mybir.AxisListType

    P = 128
    BATCHES, SEQ, D = x.shape
    OUTS = weight.shape[0]
    ADAPTERS = wq.shape[0]
    RANK = lora_a.shape[2]
    KB = D // P
    BLOCKS = BATCHES * SEQ // P
    PER_BATCH = SEQ // P
    HALF = OUTS // 2
    TILE = 512
    ROWS = HALF // P
    PIECE = 1024
    PIECES = D // PIECE * ADAPTERS
    WQ_SLOTS = 4
    GROUP = 4
    GROUPS = KB // GROUP
    TR_BANKS, ACC_BANKS = 4, 2
    GP = 256
    STACK = 4 * RANK + 2
    EXP_MASK = 0x7F800000
    SCALE_BITS, INV_BITS = float((2 * 127 + 14) << 23), float((2 * 127) << 23)
    MAX_BITS, MIN_BITS = float(253 << 23), float(1 << 23)

    x_v = x.rearrange("b (t p) i -> (b t) p i", p=P)
    out_v = out.rearrange("b (t p) o -> (b t) p o", p=P)
    w_v = weight.rearrange("(r p) i -> r p i", p=P)
    wq_v = wq.rearrange("a (r p) i -> a r p i", p=P)
    a_v = lora_a.rearrange("n (k p) r -> n p k r", p=P)

    g_dram = nc.dram_tensor("g_stack", (BATCHES, 4 * RANK, OUTS), F32).ap()
    gb_dram = nc.dram_tensor("bias_stack", (2, OUTS), F32).ap()
    bt_dram = nc.dram_tensor("b_parts", (BATCHES + 1, P, KB * 2 * RANK), F16).ap()
    a_dram = nc.dram_tensor("a_parts", (P, 2 * KB * P), F16).ap()

    ctx = ExitStack()
    with ctx:
        def sb(name, shape, dt):
            return ctx.enter_context(nc.sbuf_tensor(name, shape, dt))

        def sem(name):
            return ctx.enter_context(nc.semaphore(name))

        vt0 = sb("vt0", [P, 2, KB, HALF], F16)
        half1 = sb("half1", [P, 2 * KB * HALF], F16)
        vt1 = half1[:].rearrange("p (s k o) -> p s k o", s=2, k=KB)
        vt = [vt0, vt1]
        space = half1[:].bitcast(F32)
        a_nat = space[:, 0:D].rearrange("p (k c) -> p k c", k=KB)
        a_abs = space[:, D:2 * D].rearrange("p (k c) -> p k c", k=KB)
        b_nat = space[:, 2 * D:3 * D]
        a_first = half1[:, 6 * D:8 * D].rearrange("p (s k c) -> p s k c", s=2, k=KB)
        bt_all = half1[:, 8 * D:10 * D].rearrange("p (b k c) -> p b k c", b=BATCHES, k=KB)
        xt = sb("xt", [P, 2, 2, KB, P], F16)
        x_nat = sb("x_nat", [P, D], F32)
        wq_sb = sb("wq_sb", [P, WQ_SLOTS, PIECE], I32)
        a_again = wq_sb[:].rearrange("p s c -> p (s c)").bitcast(F16)[:, 0:2 * D].rearrange(
            "p (s k c) -> p s k c", s=2, k=KB)
        v_nat = sb("v_nat", [P, D], F32)
        junk = sb("junk", [P, PIECE], BF16)
        g_f = sb("g_f", [P, GP], F32)
        g_hi = sb("g_hi", [P, GP], F32R)
        g_lo = sb("g_lo", [P, GP], F32R)
        g_st = sb("g_st", [STACK, OUTS], F32R)
        v_inv = sb("v_inv", [P, OUTS], BF16)
        out_sb = sb("out_sb", [P, 2, TILE], F32)
        bt = sb("bt", [P, KB, 2 * RANK], F16)
        ident = sb("ident", [P, P], F32)
        ones = sb("ones", [P, P], F32)
        diag = sb("diag", [P, P], F32)
        t_lo = sb("t_lo", [P, RANK], F32)
        t_f = sb("t_f", [P, RANK], F32)
        t_st = sb("t_st", [P, STACK], F32R)
        t_t = sb("t_t", [STACK, P], F32R)
        b_pair = sb("b_pair", [P, 2], F32R)
        b_row = sb("b_row", [2, P], F32R)
        ids_sb = sb("ids_sb", [1, BATCHES], I32)
        small = sb("small", [P, 4, ADAPTERS], F32)
        zp_i = sb("zp_i", [P, ADAPTERS], I32)
        bq_i = sb("bq_i", [P, P], I32)
        bq_f = sb("bq_f", [P, P], F32)
        bias_rows = sb("bias_rows", [OUTS // P, P], F32)
        coef = sb("coef", [P, 2, ADAPTERS], F32)
        zprod = sb("zprod", [P, ADAPTERS], F32)
        c0 = sb("c0", [P, 1], F32)
        b_col = sb("b_col", [P, OUTS // P], F32)
        sums = sb("sums", [P, 8], F32)
        tot = sb("tot", [P, 1], F32)
        bits = sb("bits", [P, 1], F32)
        x_sc = sb("x_sc", [P, 2, 2], F32)
        v_sc = sb("v_sc", [P, 3], F32)
        a_sc = sb("a_sc", [P, 2], F32)
        b_sc = sb("b_sc", [P, 2], F32)
        b_tmp = sb("b_tmp", [P, 1], F32)

        acc = [ctx.enter_context(nc.psum_tensor(f"acc{i}", [P, TILE], F32)) for i in range(ACC_BANKS)]
        tr = [ctx.enter_context(nc.psum_tensor(f"tr{i}", [P, TILE], F32)) for i in range(TR_BANKS)]
        g_ps = ctx.enter_context(nc.psum_tensor("g_ps", [P, TILE], F32))
        misc = ctx.enter_context(nc.psum_tensor("misc", [P, TILE], F32))
        t_ps = misc[:, 0:2 * RANK]
        tt_ps = misc[0:STACK, 32:160]
        asum_ps = misc[:, 416:417]
        inv_ps, brow_ps = g_ps[:, 0:128], g_ps[0:2, 128:256]
        bq_ps, bias_ps, abc_ps = g_ps[:, 0:128], g_ps[:, 128:144], g_ps[:, 256:384]

        ids_in, small_in, a_in, b_in, x_in, w_in = map(sem, ("ids_in", "small_in", "a_in", "b_in", "x_in", "w_in"))
        wq_in = [sem(f"wq_in{s}") for s in range(WQ_SLOTS)]
        ident_ok, coef_ok, bq_ok, bqt_ok = map(sem, ("ident_ok", "coef_ok", "bq_ok", "bqt_ok"))
        b_abs, b_scale, b_scaled = map(sem, ("b_abs", "b_scale", "b_scaled"))
        a_absd, a_sum, a_diag, a_bc, a_scaled, a_hi, a_lo = map(
            sem, ("a_absd", "a_sum", "a_diag", "a_bc", "a_scaled", "a_hi", "a_lo"))
        bt_out, bt_in, a_out, a_back = map(sem, ("bt_out", "bt_in", "a_out", "a_back"))
        wq_used, v_sum, v_abs, v_scale, v_scaled, v_diag, v_bc, v_row, gb_out = map(
            sem, ("wq_used", "v_sum", "v_abs", "v_scale", "v_scaled", "v_diag", "v_bc", "v_row", "gb_out"))
        x_abs, x_scale, x_scaled = map(sem, ("x_abs", "x_scale", "x_scaled"))
        tr_done, hi_done, tr_free = map(sem, ("tr_done", "hi_done", "tr_free"))
        t_done, t_split, tt_done, tt_ok = map(sem, ("t_done", "t_split", "tt_done", "tt_ok"))
        g_done, g_free, g_ok, g_out, gs_in = map(sem, ("g_done", "g_free", "g_ok", "g_out", "gs_in"))
        tile_done, acc_free = map(sem, ("tile_done", "acc_free"))
        out_free = [sem("out_free0"), sem("out_free1")]

        SETUP_GROUPS = GROUPS * (1 + 1 + ROWS)
        NB = BATCHES // 2

        class Phase:
            def __init__(self, first, batches, chunks, before, rows):
                self.first, self.batches, self.chunks, self.rows = first, batches, chunks, rows
                self.c = len(chunks)
                if self.c == 2:
                    self.at = {(0, 12): "x", (1, 2): "x", (1, 6): "x", (1, 10): "x"}
                else:
                    self.at = {(1, 4): "x", (1, 12): "x", (2, 4): "x", (2, 12): "x"}
                self.tiles = PER_BATCH * self.c
                self.groups = PER_BATCH * GROUPS + rows * GROUPS
                self.q0, self.n0, self.g0, self.s0 = before

            def after(self):
                return (self.q0 + self.batches * PER_BATCH, self.n0 + self.batches * self.tiles,
                        self.g0 + self.batches * self.groups, self.s0 + self.batches)

            def jobs(self, j, ci):
                at = dict(self.at)
                if self.rows and j % 2 == 1 and ci == 1:
                    at.update({(1, 4): "v", (1, 8): "v", (1, 12): "v", (1, 14): "v"})
                found = []
                per_block = [self.per_block(i) for i in range(j)]
                base = sum(per_block)
                order = sorted(at.items())
                seen = {"x": 0, "v": 0}
                for n, ((c, k), kind) in enumerate(order):
                    if c == ci:
                        found.append((k, kind, seen[kind], base + n))
                    seen[kind] += 1
                return found

            def per_block(self, j):
                return GROUPS * (2 if self.rows and j % 2 == 1 else 1)

        p2 = Phase(0, NB, (0, 1), (0, 0, SETUP_GROUPS, 0), 2)
        p3 = Phase(NB, BATCHES - NB, (0, 1, 2, 3), p2.after(), 0)
        p4 = Phase(0, NB, (2, 3), p3.after(), 0)
        assert NB * p2.rows == ROWS

        block = ctx.enter_context(nc.Block())

        def group_view(bank):
            return bank[:].rearrange("p (m c) -> p m c", m=GROUP)

        @block.sync
        def _(sp):
            def load_row(r, first):
                if not first:
                    sp.wait_ge(v_row, r)
                sp.dma_start(v_nat[:], w_v[bass.ds(r, 1)].rearrange("r p i -> (r p) i")).then_inc(w_in, 16)
                for n in range(PIECES):
                    a, h = n // 2, n % 2
                    if not (first and n < WQ_SLOTS):
                        sp.wait_ge(wq_used, r * PIECES + n - WQ_SLOTS + 1)
                    sp.dma_start(wq_sb[:, n % WQ_SLOTS, :],
                                 wq_v[a, bass.ds(r, 1), :, h * PIECE:(h + 1) * PIECE].rearrange(
                                     "r p i -> (r p) i")).then_inc(wq_in[n % WQ_SLOTS], 16)

            def store_g(half):
                for piece in range(HALF // GP):
                    n = half * (HALF // GP) + piece
                    sp.wait_ge(g_ok, n + 1)
                    for dup in range(2):
                        for part, src in enumerate((g_hi, g_lo)):
                            r0 = (2 * part + dup) * RANK
                            sp.dma_start(g_dram[:, r0:r0 + RANK, n * GP:(n + 1) * GP],
                                         src[:].bitcast(F32)).then_inc(g_out, 16)

            sp.dma_start(ids_sb[:], ids.rearrange("(a b) -> a b", a=1)).then_inc(ids_in, 16)
            sp.wait_ge(ids_in, 16)
            for b in range(BATCHES):
                n = sp.value_load(ids_sb[0:1, b:b + 1], min_val=0, max_val=lora_a.shape[0] - 1)
                sp.dma_start(b_nat[b * RANK:(b + 1) * RANK, :],
                             lora_b[bass.ds(n, 1)].rearrange("n r i -> (n r) i")).then_inc(b_in, 16)
                sp.dma_start(a_nat[:, :, b * RANK:(b + 1) * RANK],
                             a_v[bass.ds(n, 1)].rearrange("n p k r -> (n p) k r")).then_inc(a_in, 16)
            load_row(0, True)
            with sp.Fori(1, ROWS) as r:
                load_row(r, False)
            sp.wait_ge(a_hi, 1)
            sp.wait_ge(a_lo, 1)
            sp.dma_start(a_dram, half1[:, 6 * D:8 * D]).then_inc(a_out, 16)
            store_g(0)
            sp.wait_ge(a_out, 16)
            with sp.Fori(ROWS, 2 * ROWS) as r:
                load_row(r, False)
            sp.wait_ge(wq_used, 2 * ROWS * PIECES)
            sp.dma_start(wq_sb[:].rearrange("p s c -> p (s c)").bitcast(F16)[:, 0:2 * D],
                         a_dram).then_inc(a_back, 16)
            store_g(1)
            sp.wait_ge(g_out, 16 * 4 * OUTS // GP)

        @block.gpsimd
        def _(pool):
            pool.memset(ones[:], 1.0).then_inc(tile_done, 1)
            pool.memset(ident[:], 0.0).then_inc(ident_ok, 1)
            pool.wait_ge(ident_ok, 1)
            pool.affine_select(out=ident[:], in_=ident[:], compare_op=ALU.not_equal, fill=1.0, base=0,
                               pattern=[[-1, P]], channel_multiplier=1).then_inc(ident_ok, 1)

            bt_flat = bt[:].rearrange("p k c -> p (k c)")

            def load_bt(b):
                pool.dma_start(bt_flat, bt_dram[bass.ds(b, 1)].rearrange("b p c -> (b p) c")).then_inc(bt_in, 16)

            pool.wait_ge(bt_out, 32)
            load_bt(0)

            def phase(ph):
                cols = slice(ph.chunks[0] * TILE, (ph.chunks[-1] + 1) * TILE)
                pool.wait_ge(g_out, 16 * 4 * ((ph.chunks[-1] + 1) * TILE // GP))
                pool.wait_ge(gb_out, 16 * (ph.chunks[-1] + 1) * TILE // P)
                with pool.Fori(0, ph.batches) as it:
                    b = it + ph.first
                    n = ph.n0 + it * ph.tiles
                    pool.wait_ge(tile_done, n + 1)
                    pool.dma_start(g_st[0:4 * RANK, cols].bitcast(F32), g_dram[bass.ds(b, 1), :, cols].rearrange(
                        "b r o -> (b r) o")).then_inc(gs_in, 16)
                    pool.dma_start(g_st[4 * RANK:STACK, cols].bitcast(F32), gb_dram[:, cols]).then_inc(gs_in, 16)
                    for j in range(PER_BATCH):
                        for ci, c in enumerate(ph.chunks):
                            t = j * ph.c + ci
                            pool.wait_ge(acc_free, n + t + ACC_BANKS + 1)
                            pool.dma_start(
                                out_v[bass.ds(b * PER_BATCH + j, 1), :, c * TILE:(c + 1) * TILE].rearrange(
                                    "t p o -> (t p) o"), out_sb[:, t % 2, :]).then_inc(out_free[t % 2], 16)
                            if j == PER_BATCH - 1 and ci == 0:
                                pool.wait_ge(t_done, ph.q0 + it * PER_BATCH + PER_BATCH)
                                load_bt(b + 1)

            phase(p2)
            phase(p3)
            phase(p4)
            last = p4.after()[1]
            for s in range(2):
                pool.wait_ge(out_free[s], 16 * (last // 2))
            pool.wait_ge(bt_in, 16 * (p4.after()[3] + 1))

        @block.scalar
        def _(act):
            def load_x(blk):
                act.dma_start(x_nat[:], x_v[bass.ds(blk, 1)].rearrange("t p i -> (t p) i")).then_inc(x_in, 16)

            def abs_sums(src, col, done):
                for h in range(2):
                    if h:
                        act.drain()
                    s = act.activation(junk[:], src[:, h * PIECE:(h + 1) * PIECE], ACT.Abs,
                                       bias=c0[:] if done is v_abs else 0.0,
                                       accum_out=sums[:, col + h:col + h + 1])
                s.then_inc(done, 1)

            def hi(g, bank, dst):
                act.wait_ge(tr_done, g + 1)
                act.activation(dst, group_view(tr[bank]), ACT.Copy).then_inc(hi_done, 1)

            def v_prepare(r):
                act.drain()
                act.wait_ge(v_sum, r + 1)
                abs_sums(v_nat, 2, v_abs)
                act.wait_ge(v_scale, r + 1)
                act.activation(v_nat[:], v_nat[:], ACT.Identity, bias=v_sc[:, 2:3],
                               scale=v_sc[:, 0:1]).then_inc(v_scaled, 1)

            def v_hi(half, r, m, g, bank):
                o = (r - half * ROWS) * P
                hi(g, bank, vt[half][:, 0, m * GROUP:(m + 1) * GROUP, bass.ds(o, P)])

            def v_rows(r, first=False):
                act.wait_ge(v_bc, r + 1)
                act.activation(v_inv[:, bass.ds(r * P, P)], inv_ps, ACT.Copy)
                if not first:
                    act.wait_ge(gb_out, 16 * r)
                act.activation(b_row[:], brow_ps, ACT.Copy).then_inc(v_row, 1)
                act.wait_ge(v_row, r + 1)
                act.dma_start(gb_dram[:, bass.ds(r * P, P)], b_row[:].bitcast(F32)).then_inc(gb_out, 16)

            def x_prepare(q, slot):
                act.drain()
                act.wait_ge(x_in, 16 * (q + 1))
                abs_sums(x_nat, 0, x_abs)
                act.wait_ge(x_scale, q + 1)
                act.activation(x_nat[:], x_nat[:], ACT.Copy, scale=x_sc[:, slot, 0:1]).then_inc(x_scaled, 1)

            def x_hi(slot, m, g, bank):
                hi(g, bank, xt[:, slot, 0, m * GROUP:(m + 1) * GROUP, :])

            for i, src in enumerate((scale, wscale, bscale)):
                act.dma_start(small[:, i, :], src.rearrange("(o a) -> o a", o=1).to_broadcast([P, ADAPTERS])
                              ).then_inc(small_in, 16)
            act.dma_start(zp_i[:], zp.rearrange("(o a) -> o a", o=1).to_broadcast([P, ADAPTERS])).then_inc(small_in, 16)
            act.dma_start(bq_i[:], bq.rearrange("a (r p) -> (a r) p", p=P)).then_inc(small_in, 16)
            act.dma_start(bias_rows[:], bias.rearrange("(r p) -> r p", p=P)).then_inc(small_in, 16)
            load_x(0)
            act.wait_ge(b_in, 16 * BATCHES)
            abs_sums(b_nat, 4, b_abs)
            act.wait_ge(b_scale, 1)
            act.activation(b_nat, b_nat, ACT.Copy, scale=b_sc[:, 0:1]).then_inc(b_scaled, 1)
            for m in range(GROUPS):
                act.wait_ge(tr_done, m + 1)
                act.activation(bt_all[:, :, m * GROUP:(m + 1) * GROUP, RANK:].rearrange("p b k r -> p k b r"),
                               tr[m][:].rearrange("p (k b r) -> p k b r", k=GROUP, b=BATCHES),
                               ACT.Copy).then_inc(hi_done, 1)
            act.wait_ge(tr_free, TR_BANKS + GROUPS)
            act.dma_start(bt_dram[0:BATCHES].rearrange("b p c -> p b c"),
                          bt_all.rearrange("p b k c -> p b (k c)")).then_inc(bt_out, 16)
            act.dma_start(bt_dram[BATCHES], bt_all[:, 0].rearrange("p k c -> p (k c)")).then_inc(bt_out, 16)
            act.wait_ge(a_in, 16 * BATCHES)
            act.activation(a_abs, a_nat, ACT.Abs).then_inc(a_absd, 1)
            act.wait_ge(a_scaled, 1)
            act.activation(a_first[:, 0], a_nat, ACT.Copy).then_inc(a_hi, 1)
            x_prepare(0, 0)
            for m in range(GROUPS):
                x_hi(0, m, GROUPS + m, m % TR_BANKS)
            load_x(1)
            v_prepare(0)
            for m in range(GROUPS):
                v_hi(0, 0, m, 2 * GROUPS + m, m % TR_BANKS)
            v_rows(0, True)
            with act.Fori(1, ROWS) as r:
                v_prepare(r)
                for m in range(GROUPS):
                    v_hi(0, r, m, 2 * GROUPS + r * GROUPS + m, m % TR_BANKS)
                v_rows(r)

            def batch(ph, it, loads):
                q0, g0 = ph.q0 + it * PER_BATCH, ph.g0 + it * ph.groups
                for j in range(PER_BATCH):
                    q = q0 + j
                    for ci in range(ph.c):
                        if ci == 0:
                            x_prepare(q + 1, (j + 1) % 2)
                            act.wait_ge(tt_done, q + 1)
                            act.activation(t_t[:], tt_ps, ACT.Copy).then_inc(tt_ok, 1)
                        r = ROWS + it * 2 + j // 2
                        for k, kind, m, g in ph.jobs(j, ci):
                            if kind == "x":
                                x_hi((j + 1) % 2, m, g0 + g, g % TR_BANKS)
                                if m == GROUPS - 1:
                                    load_x(loads(q + 2))
                            else:
                                v_hi(1, r, m, g0 + g, g % TR_BANKS)
                        if ph.rows and j % 2 == 1 and ci == 0:
                            v_prepare(r)
                        if ph.rows and j % 2 == 1 and ci == 1:
                            v_rows(r)

            with act.Fori(0, p2.batches) as it:
                batch(p2, it, lambda q: q)
            with act.Fori(0, p3.batches - 1) as it:
                batch(p3, it, lambda q: q)
            batch(p3, p3.batches - 1, lambda q: q % BLOCKS)
            with act.Fori(0, p4.batches) as it:
                batch(p4, it, lambda q: q - BLOCKS)
            act.wait_ge(x_in, 16 * (p4.after()[0] + 2))

        @block.vector
        def _(dve):
            def pow2(total, s, inv):
                ti, bi = total.bitcast(I32), bits[:].bitcast(I32)
                dve.drain()
                dve.tensor_scalar(bi, ti, EXP_MASK, None, ALU.bitwise_and)
                dve.drain()
                dve.tensor_scalar(bi, bi, -1.0, SCALE_BITS, ALU.mult, ALU.add)
                dve.drain()
                dve.tensor_scalar(s.bitcast(I32), bi, MAX_BITS, MIN_BITS, ALU.min, ALU.max)
                dve.drain()
                return dve.tensor_scalar(inv.bitcast(I32), s.bitcast(I32), -1.0, INV_BITS, ALU.mult, ALU.add)

            def lo(g, bank, dst, part_hi):
                dve.wait_ge(hi_done, g + 1)
                dve.tensor_tensor(dst, group_view(tr[bank]), part_hi, ALU.subtract).then_inc(tr_free, 1)

            def x_pow2(q, slot):
                dve.wait_ge(x_abs, q + 1)
                dve.tensor_tensor(tot[:], sums[:, 0:1], sums[:, 1:2], ALU.add)
                pow2(tot[:], x_sc[:, slot, 0:1], x_sc[:, slot, 1:2]).then_inc(x_scale, 1)

            def x_lo(slot, m, g, bank):
                ks = slice(m * GROUP, (m + 1) * GROUP)
                lo(g, bank, xt[:, slot, 1, ks, :], xt[:, slot, 0, ks, :])

            def v_terms(r, pieces):
                for n in pieces:
                    a, h = n // 2, n % 2
                    if n == 0:
                        dve.wait_ge(w_in, 16 * (r + 1))
                    dve.wait_ge(wq_in[n % WQ_SLOTS], 16 * (r * (PIECES // WQ_SLOTS) + n // WQ_SLOTS + 1))
                    if n >= 2:
                        dve.wait_ge(wq_used, r * PIECES + n - 1)
                    dst = v_nat[:, h * PIECE:(h + 1) * PIECE]
                    dve.scalar_tensor_tensor(dst, wq_sb[:, n % WQ_SLOTS, :], coef[:, 0, a:a + 1], dst,
                                             ALU.mult, ALU.add).then_inc(wq_used, 1)
                if n == PIECES - 1:
                    dve.wait_ge(wq_used, (r + 1) * PIECES)
                    own = v_nat[:, bass.ds(r * P, P)]
                    dve.tensor_tensor(own, own, ident[:], ALU.add).then_inc(v_sum, 1)

            def v_pow2(r):
                dve.wait_ge(v_abs, r + 1)
                dve.tensor_tensor(tot[:], sums[:, 2:3], sums[:, 3:4], ALU.add)
                pow2(tot[:], v_sc[:, 0:1], v_sc[:, 1:2])
                dve.drain()
                dve.tensor_scalar(v_sc[:, 2:3], c0[:], v_sc[:, 0:1], None, ALU.mult).then_inc(v_scale, 1)
                dve.tensor_scalar(diag[:], ident[:], v_sc[:, 1:2], None, ALU.mult)
                dve.tensor_scalar(b_tmp[:], b_col[:, bass.ds(r, 1)], v_sc[:, 0:1], None, ALU.mult)
                dve.drain()
                dve.tensor_copy(b_pair[:, 0:1], b_tmp[:])
                dve.drain()
                dve.tensor_tensor(b_pair[:, 1:2], b_tmp[:], b_pair[:, 0:1].bitcast(F32),
                                  ALU.subtract).then_inc(v_diag, 1)

            def v_lo(half, r, m, g, bank):
                o = (r - half * ROWS) * P
                ks = slice(m * GROUP, (m + 1) * GROUP)
                lo(g, bank, vt[half][:, 1, ks, bass.ds(o, P)], vt[half][:, 0, ks, bass.ds(o, P)])

            def t_parts(q, slot):
                dve.wait_ge(t_done, q + 1)
                dve.tensor_copy(t_lo[:], t_ps[:, 0:RANK])
                dve.drain()
                dve.tensor_tensor(t_f[:], t_ps[:, RANK:2 * RANK], t_lo[:], ALU.add)
                dve.drain()
                parts = t_st[:, 0:4 * RANK].rearrange("p (u s r) -> p u s r", u=2, s=2)
                twice = t_f[:].rearrange("p (u r) -> p u r", u=1).to_broadcast([P, 2, RANK])
                dve.tensor_copy(parts[:, :, 0, :], twice)
                dve.tensor_copy(t_st[:, 4 * RANK:STACK], x_sc[:, slot, 0:1].to_broadcast([P, 2]))
                dve.drain()
                dve.tensor_tensor(parts[:, :, 1, :], twice, parts[:, :, 0, :].bitcast(F32),
                                  ALU.subtract).then_inc(t_split, 1)

            def evacuate(ph, it, t, c, slot):
                dve.wait_ge(tile_done, ph.n0 + it * ph.tiles + t + 2)
                stored = ph.n0 // 2 + it * (ph.tiles // 2) + t // 2
                if not (isinstance(stored, int) and stored == 0):
                    dve.wait_ge(out_free[t % 2], 16 * stored)
                dve.scalar_tensor_tensor(out_sb[:, t % 2, :], acc[t % ACC_BANKS][:], x_sc[:, slot, 1:2],
                                         v_inv[:, c * TILE:(c + 1) * TILE], ALU.mult, ALU.mult
                                         ).then_inc(acc_free, 1)

            def g_parts(half):
                for piece in range(HALF // GP):
                    n = half * (HALF // GP) + piece
                    at = piece % (TILE // GP) * GP
                    dve.wait_ge(g_done, n // (TILE // GP) + 1)
                    if n:
                        dve.wait_ge(g_out, 16 * 4 * n)
                    dve.tensor_scalar(g_f[:], g_ps[:, at:at + GP], a_sc[:, 1:2], b_sc[:, 1:2],
                                      ALU.mult, ALU.mult).then_inc(g_free, 1)
                    dve.drain()
                    dve.tensor_copy(g_hi[:], g_f[:])
                    dve.drain()
                    dve.tensor_tensor(g_lo[:], g_f[:], g_hi[:].bitcast(F32), ALU.subtract).then_inc(g_ok, 1)

            dve.memset(tot[:], 0.0).then_inc(tr_free, TR_BANKS)
            dve.memset(bits[:], 0.0).then_inc(acc_free, ACC_BANKS)
            dve.wait_ge(small_in, 16 * 6)
            dve.tensor_copy(small[:, 3, :], zp_i[:])
            dve.tensor_copy(bq_f[:], bq_i[:]).then_inc(bq_ok, 1)
            dve.tensor_tensor(coef[:, 0, :], small[:, 0, :], small[:, 1, :], ALU.mult)
            dve.tensor_tensor(coef[:, 1, :], small[:, 0, :], small[:, 2, :], ALU.mult)
            dve.drain()
            dve.tensor_tensor(zprod[:], small[:, 0, :], small[:, 3, :], ALU.mult)
            dve.drain()
            dve.tensor_reduce(c0[:], zprod[:], AX.X, ALU.add)
            dve.drain()
            dve.wait_ge(bqt_ok, 1)
            dve.tensor_scalar(b_col[:], bias_ps, c0[:], None, ALU.add)
            for a in range(ADAPTERS):
                dve.drain()
                dve.scalar_tensor_tensor(b_col[:], bq_ps[:, a * KB:(a + 1) * KB], coef[:, 1, a:a + 1], b_col[:],
                                         ALU.mult, ALU.add)
            dve.drain()
            dve.wait_ge(b_abs, 1)
            dve.tensor_tensor(tot[:], sums[:, 4:5], sums[:, 5:6], ALU.add)
            pow2(tot[:], b_sc[:, 0:1], b_sc[:, 1:2]).then_inc(b_scale, 1)
            for m in range(GROUPS):
                ks = slice(m * GROUP, (m + 1) * GROUP)
                dve.wait_ge(hi_done, m + 1)
                dve.tensor_tensor(bt_all[:, :, ks, 0:RANK].rearrange("p b k r -> p k b r"),
                                  tr[m][:].rearrange("p (k b r) -> p k b r", k=GROUP, b=BATCHES),
                                  bt_all[:, :, ks, RANK:].rearrange("p b k r -> p k b r"),
                                  ALU.subtract).then_inc(tr_free, 1)
            dve.wait_ge(a_sum, 1)
            dve.tensor_copy(sums[:, 6:7], asum_ps)
            pow2(sums[:, 6:7], a_sc[:, 0:1], a_sc[:, 1:2])
            dve.drain()
            dve.tensor_scalar(diag[:], ident[:], a_sc[:, 0:1], None, ALU.mult).then_inc(a_diag, 1)
            dve.wait_ge(a_bc, 1)
            spread = abc_ps.rearrange("p (k c) -> p k c", k=1).to_broadcast([P, KB, P])
            dve.tensor_tensor(a_nat, a_nat, spread, ALU.mult).then_inc(a_scaled, 1)
            dve.wait_ge(a_hi, 1)
            dve.tensor_tensor(a_first[:, 1], a_nat, a_first[:, 0], ALU.subtract).then_inc(a_lo, 1)
            x_pow2(0, 0)
            for m in range(GROUPS):
                x_lo(0, m, GROUPS + m, m % TR_BANKS)
            with dve.Fori(0, ROWS) as r:
                v_terms(r, range(PIECES))
                v_pow2(r)
                for m in range(GROUPS):
                    v_lo(0, r, m, 2 * GROUPS + r * GROUPS + m, m % TR_BANKS)
            g_parts(0)

            def batch(ph, it):
                q0, g0 = ph.q0 + it * PER_BATCH, ph.g0 + it * ph.groups
                for j in range(PER_BATCH):
                    for ci, c in enumerate(ph.chunks):
                        t = j * ph.c + ci
                        if t:
                            evacuate(ph, it, t - 1, ph.chunks[(ci - 1) % ph.c], (j - (ci == 0)) % 2)
                        if ci == 0:
                            t_parts(q0 + j, j % 2)
                            x_pow2(q0 + j + 1, (j + 1) % 2)
                        r = ROWS + it * 2 + j // 2
                        if ph.rows:
                            share = (range(0, 6), range(6, 12), range(12, PIECES), ())[(j % 2) * 2 + ci]
                            if len(share):
                                v_terms(r, share)
                        for k, kind, m, g in ph.jobs(j, ci):
                            if kind == "x":
                                x_lo((j + 1) % 2, m, g0 + g, g % TR_BANKS)
                            else:
                                v_lo(1, r, m, g0 + g, g % TR_BANKS)
                        if ph.rows and (j % 2) * 2 + ci == 2:
                            v_pow2(r)
                evacuate(ph, it, ph.tiles - 1, ph.chunks[-1], (PER_BATCH - 1) % 2)

            batch(p2, 0)
            with dve.Fori(1, p2.batches) as it:
                batch(p2, it)
            g_parts(1)
            with dve.Fori(0, p3.batches) as it:
                batch(p3, it)
            with dve.Fori(0, p4.batches) as it:
                batch(p4, it)

        @block.tensor
        def _(pe):
            def group(g, bank, src, m):
                pe.wait_ge(tr_free, g + 1)
                for i in range(GROUP):
                    k = m * GROUP + i
                    last = pe.transpose(tr[bank][:, i * P:(i + 1) * P], src[:, k * P:(k + 1) * P], ident[:])
                last.then_inc(tr_done, 1)

            def v_spread(r):
                pe.wait_ge(v_diag, r + 1)
                pe.matmul(inv_ps, ones[:], diag[:], start=True, stop=True)
                pe.transpose(brow_ps, b_pair[:].bitcast(F32), ident[:]).then_inc(v_bc, 1)

            def g_product(half):
                a_parts = a_first if half == 0 else a_again
                pe.wait_ge(v_row, (half + 1) * ROWS)
                pe.wait_ge(tr_free, TR_BANKS + (SETUP_GROUPS if half == 0 else p3.g0))
                if half:
                    pe.wait_ge(a_back, 16)
                else:
                    pe.wait_ge(a_lo, 1)
                for c in range(HALF // TILE):
                    n = half * (HALF // TILE) + c
                    if n:
                        pe.wait_ge(g_free, n * (TILE // GP))
                    for k in range(KB):
                        for s, (pa, pv) in enumerate(((0, 0), (0, 1), (1, 0))):
                            last = pe.matmul(g_ps[:], a_parts[:, pa, k, :],
                                             vt[half][:, pv, k, c * TILE:(c + 1) * TILE],
                                             start=(k == 0 and s == 0), stop=(k == KB - 1 and s == 2))
                    last.then_inc(g_done, 1)

            pe.wait_ge(ident_ok, 2)
            pe.wait_ge(bq_ok, 1)
            pe.transpose(bq_ps, bq_f[:], ident[:])
            pe.transpose(bias_ps, bias_rows[:], ident[0:OUTS // P, 0:OUTS // P]).then_inc(bqt_ok, 1)
            pe.wait_ge(b_scaled, 1)
            for m in range(GROUPS):
                group(m, m, b_nat, m)
            pe.wait_ge(a_absd, 1)
            for k in range(KB):
                last = pe.matmul(asum_ps, a_abs[:, k, :], ones[:, 0:1], start=(k == 0), stop=(k == KB - 1))
            last.then_inc(a_sum, 1)
            pe.wait_ge(a_diag, 1)
            pe.matmul(abc_ps, ones[:], diag[:], start=True, stop=True).then_inc(a_bc, 1)
            pe.wait_ge(x_scaled, 1)
            for m in range(GROUPS):
                group(GROUPS + m, m % TR_BANKS, x_nat, m)
            with pe.Fori(0, ROWS) as r:
                pe.wait_ge(v_scaled, r + 1)
                for m in range(GROUPS):
                    group(2 * GROUPS + r * GROUPS + m, m % TR_BANKS, v_nat, m)
                v_spread(r)
            g_product(0)

            def batch(ph, it):
                n = ph.n0 + it * ph.tiles
                q0, g0 = ph.q0 + it * PER_BATCH, ph.g0 + it * ph.groups
                for j in range(PER_BATCH):
                    slot = j % 2
                    if j == 0:
                        pe.wait_ge(bt_in, 16 * (ph.s0 + it + 1))
                    x_last = max(g for ci in range(ph.c) for _, kind, _, g in ph.jobs(j, ci) if kind == "x")
                    done = g0 + sum(ph.per_block(i) for i in range(j))
                    pe.wait_ge(tr_free, TR_BANKS + done)
                    for k in range(KB):
                        pe.matmul(t_ps, xt[:, slot, 0, k, :], bt[:, k, :], start=(k == 0), stop=False)
                        last = pe.matmul(t_ps[:, RANK:], xt[:, slot, 1, k, :], bt[:, k, RANK:],
                                         start=False, stop=(k == KB - 1))
                    last.then_inc(t_done, 1)
                    for ci, c in enumerate(ph.chunks):
                        t = j * ph.c + ci
                        jobs = {k: (kind, m, g) for k, kind, m, g in ph.jobs(j, ci)}
                        bank = acc[t % ACC_BANKS]
                        half, col = c * TILE // HALF, c * TILE % HALF
                        pe.wait_ge(acc_free, n + t + 1)
                        for k in range(KB):
                            if k in jobs:
                                kind, m, g = jobs[k]
                                if kind == "x" and m == 0:
                                    pe.wait_ge(x_scaled, q0 + j + 2)
                                if kind == "v" and m == 0:
                                    pe.wait_ge(v_scaled, ROWS + it * 2 + j // 2 + 1)
                                group(g0 + g, g % TR_BANKS, x_nat if kind == "x" else v_nat, m)
                            if ci == 0 and k == KB // 2:
                                pe.wait_ge(t_split, q0 + j + 1)
                                pe.transpose(tt_ps, t_st[:].bitcast(F32), ident[:]).then_inc(tt_done, 1)
                            for s, (px, pv) in enumerate(((0, 0), (0, 1), (1, 0))):
                                pe.matmul(bank[:], xt[:, slot, px, k, :], vt[half][:, pv, k, col:col + TILE],
                                          start=(k == 0 and s == 0), stop=False)
                        if ph.rows and j % 2 == 1 and ci == 1:
                            v_spread(ROWS + it * 2 + j // 2)
                        if ci == 0:
                            pe.wait_ge(tt_ok, q0 + j + 1)
                            if j == 0:
                                pe.wait_ge(gs_in, 32 * (ph.s0 + it + 1))
                        pe.matmul(bank[:], t_t[:], g_st[:, c * TILE:(c + 1) * TILE],
                                  start=False, stop=True).then_inc(tile_done, 1)

            with pe.Fori(0, p2.batches) as it:
                batch(p2, it)
            g_product(1)
            with pe.Fori(0, p3.batches) as it:
                batch(p3, it)
            with pe.Fori(0, p4.batches) as it:
                batch(p4, it)


def kernel(x, itok_B_4_50, condB_scale, itok_Bx4096x4096_0_255, condB_wscale, itok_Bx4096_0_255,
           condB_bscale, _lenS, L0_cond_A, L0_cond_B, L1_cond_weight, L1_cond_bias):
    import numpy as np
    from concourse import bacc, mybir
    from concourse.bass_utils import run_bass_kernel_spmd

    nc = bacc.Bacc("TRN2", target_bir_lowering=False, num_devices=1)
    given = {
        "x": x, "ids": itok_B_4_50, "scale": condB_scale, "wq": itok_Bx4096x4096_0_255,
        "wscale": condB_wscale, "bq": itok_Bx4096_0_255, "bscale": condB_bscale, "zp": _lenS,
        "lora_a": L0_cond_A, "lora_b": L0_cond_B, "weight": L1_cond_weight, "bias": L1_cond_bias,
    }
    arrays, aps = {}, {}
    for name, a in given.items():
        a = np.ascontiguousarray(a)
        arrays[f"in_{name}"] = a
        aps[name] = nc.dram_tensor(f"in_{name}", a.shape, mybir.dt.from_np(a.dtype), kind="ExternalInput").ap()
    aps["out"] = nc.dram_tensor("out_0", arrays["in_x"].shape, mybir.dt.float32, kind="ExternalOutput").ap()
    build_program(nc, **aps)
    r = run_bass_kernel_spmd(nc, [arrays], core_ids=[0])
    return r.results[0]["out_0"]
```

```python
def build_program(nc, x, ids, scale, wq, wscale, bq, bscale, zp, lora_a, lora_b, weight, bias, out):
    import concourse.bass as bass
    from concourse import mybir
    from contextlib import ExitStack

    F32, F32R, F16 = mybir.dt.float32, mybir.dt.float32r, mybir.dt.float16
    BF16, I32 = mybir.dt.bfloat16, mybir.dt.int32
    ALU, ACT, AX = mybir.AluOpType, mybir.ActivationFunctionType, mybir.AxisListType

    P = 128
    BATCHES, SEQ, D = x.shape
    OUTS = weight.shape[0]
    ADAPTERS = wq.shape[0]
    RANK = lora_a.shape[2]
    KB = D // P
    BLOCKS = BATCHES * SEQ // P
    PER_BATCH = SEQ // P
    HALF = OUTS // 2
    TILE = 512
    ROWS = HALF // P
    PIECE = 1024
    PIECES = D // PIECE * ADAPTERS
    WQ_SLOTS = 4
    GROUP = 4
    GROUPS = KB // GROUP
    TR_BANKS, ACC_BANKS = 4, 2
    GP = 256
    FIRST = 8
    STEPS = HALF // GP
    STACK = 4 * RANK + 2
    EXP_MASK = 0x7F800000
    SCALE_BITS, INV_BITS = float((2 * 127 + 14) << 23), float((2 * 127) << 23)
    MAX_BITS, MIN_BITS = float(253 << 23), float(1 << 23)

    x_v = x.rearrange("b (t p) i -> (b t) p i", p=P)
    out_v = out.rearrange("b (t p) o -> (b t) p o", p=P)
    w_v = weight.rearrange("(r p) i -> r p i", p=P)
    wq_v = wq.rearrange("a (r p) i -> a r p i", p=P)
    a_v = lora_a.rearrange("n (k p) r -> n p k r", p=P)

    g_dram = nc.dram_tensor("g_stack", (BATCHES, 4 * RANK, OUTS), F32).ap()
    gb_dram = nc.dram_tensor("bias_stack", (2, OUTS), F32).ap()
    KEPT = 3 * BLOCKS // 4
    xt_dram = nc.dram_tensor("xt_parts", (KEPT, P, 2 * KB * P), F16).ap()
    tt_dram = nc.dram_tensor("t_stack", (KEPT, STACK, P), F32).ap()
    bt_dram = nc.dram_tensor("b_parts", (BATCHES, P, KB * 2 * RANK), F16).ap()
    a_dram = nc.dram_tensor("a_parts", (P, 2 * KB * P), F16).ap()

    ctx = ExitStack()
    with ctx:
        def sb(name, shape, dt):
            return ctx.enter_context(nc.sbuf_tensor(name, shape, dt))

        def sem(name):
            return ctx.enter_context(nc.semaphore(name))

        vt0 = sb("vt0", [P, 2, KB, HALF], F16)
        half1 = sb("half1", [P, 2 * KB * HALF], F16)
        vt1 = half1[:].rearrange("p (s k o) -> p s k o", s=2, k=KB)
        vt = [vt0, vt1]
        space = half1[:].bitcast(F32)
        a_nat = space[:, 0:D].rearrange("p (k c) -> p k c", k=KB)
        a_abs = space[:, D:2 * D].rearrange("p (k c) -> p k c", k=KB)
        b_nat = space[:, 2 * D:3 * D]
        bt_all = half1[:, 6 * D:8 * D].rearrange("p (b k c) -> p b k c", b=BATCHES, k=KB)
        x_nat = sb("x_nat", [P, D], F32)
        xt = sb("xt", [P, 2, 2, KB, P], F16)
        xt_more = half1[:, 0:12 * D].rearrange("p (b s k c) -> p b s k c", b=6, s=2, k=KB)
        xt_first = [xt[:, 0], xt[:, 1]] + [xt_more[:, i] for i in (4, 5, 3, 2, 1, 0)]
        x_places = [x_nat[:], space[:, 5 * D:6 * D], x_nat[:], space[:, 0:D]]
        x_places += [x_nat[:], space[:, 0:D], x_nat[:], x_nat[:], x_nat[:]]
        X_OTHER = (1, 3, 5)
        v_other = space[:, 6 * D:7 * D]
        a_first = half1[:, 14 * D:16 * D].rearrange("p (s k c) -> p s k c", s=2, k=KB)
        wq_sb = sb("wq_sb", [P, WQ_SLOTS, PIECE], I32)
        a_again = wq_sb[:].rearrange("p s c -> p (s c)").bitcast(F16)[:, 0:2 * D].rearrange(
            "p (s k c) -> p s k c", s=2, k=KB)
        v_nat = sb("v_nat", [P, D], F32)
        junk = sb("junk", [P, PIECE], BF16)
        g_f = sb("g_f", [P, GP], F32)
        g_hi = sb("g_hi", [P, GP], F32R)
        g_lo = sb("g_lo", [P, GP], F32R)
        g_st = sb("g_st", [STACK, OUTS], F32R)
        v_inv = sb("v_inv", [P, OUTS], BF16)
        out_sb = sb("out_sb", [P, 2, TILE], F32)
        bt = sb("bt", [P, KB, 2 * RANK], F16)
        ident = sb("ident", [P, P], F32)
        ones = sb("ones", [P, P], F32)
        diag = sb("diag", [P, P], F32)
        t_lo = sb("t_lo", [P, RANK], F32)
        t_f = sb("t_f", [P, RANK], F32)
        t_st = sb("t_st", [P, STACK], F32R)
        t_t = sb("t_t", [STACK, FIRST, P], F32R)
        b_pair = sb("b_pair", [P, 2], F32R)
        b_row = sb("b_row", [2, P], F32R)
        ids_sb = sb("ids_sb", [1, BATCHES], I32)
        small = sb("small", [P, 4, ADAPTERS], F32)
        zp_i = sb("zp_i", [P, ADAPTERS], I32)
        bq_i = sb("bq_i", [P, P], I32)
        bq_f = sb("bq_f", [P, P], F32)
        bias_rows = sb("bias_rows", [OUTS // P, P], F32)
        coef = sb("coef", [P, 2, ADAPTERS], F32)
        zprod = sb("zprod", [P, ADAPTERS], F32)
        c0 = sb("c0", [P, 1], F32)
        b_col = sb("b_col", [P, OUTS // P], F32)
        sums = sb("sums", [P, 8], F32)
        tot = sb("tot", [P, 1], F32)
        bits = sb("bits", [P, 1], F32)
        x_sc = sb("x_sc", [P, FIRST, 2], F32)
        x_inv = sb("x_inv", [P, KEPT], F32)
        v_sc = sb("v_sc", [P, 3], F32)
        a_sc = sb("a_sc", [P, 2], F32)
        b_sc = sb("b_sc", [P, 2], F32)
        b_tmp = sb("b_tmp", [P, 1], F32)

        acc = [ctx.enter_context(nc.psum_tensor(f"acc{i}", [P, TILE], F32)) for i in range(ACC_BANKS)]
        tr = [ctx.enter_context(nc.psum_tensor(f"tr{i}", [P, TILE], F32)) for i in range(TR_BANKS)]
        g_ps = ctx.enter_context(nc.psum_tensor("g_ps", [P, TILE], F32))
        misc = ctx.enter_context(nc.psum_tensor("misc", [P, TILE], F32))
        t_ps = misc[:, 0:2 * RANK]
        tt_ps = misc[0:STACK, 32:160]
        asum_ps = misc[:, 416:417]
        inv_ps, brow_ps = g_ps[:, 0:128], g_ps[0:2, 128:256]
        bq_ps, bias_ps, abc_ps = g_ps[:, 0:128], g_ps[:, 128:144], g_ps[:, 256:384]

        ids_in, small_in, a_in, b_in, w_in = map(sem, ("ids_in", "small_in", "a_in", "b_in", "w_in"))
        x_in, x_in_other = map(sem, ("x_in", "x_in_other"))
        wq_in = [sem(f"wq_in{s}") for s in range(WQ_SLOTS)]
        ident_ok, coef_ok, bq_ok, bqt_ok = map(sem, ("ident_ok", "coef_ok", "bq_ok", "bqt_ok"))
        b_abs, b_scale, b_scaled = map(sem, ("b_abs", "b_scale", "b_scaled"))
        a_absd, a_sum, a_diag, a_bc, a_scaled, a_hi, a_lo = map(
            sem, ("a_absd", "a_sum", "a_diag", "a_bc", "a_scaled", "a_hi", "a_lo"))
        bt_out, bt_in, a_out, a_back = map(sem, ("bt_out", "bt_in", "a_out", "a_back"))
        wq_used, v_sum, v_abs, v_scale, v_scaled, v_diag, v_bc, v_row, gb_out = map(
            sem, ("wq_used", "v_sum", "v_abs", "v_scale", "v_scaled", "v_diag", "v_bc", "v_row", "gb_out"))
        x_abs, x_scale, x_scaled = map(sem, ("x_abs", "x_scale", "x_scaled"))
        tr_done, hi_done, tr_free = map(sem, ("tr_done", "hi_done", "tr_free"))
        t_done, t_split, tt_done, tt_ok = map(sem, ("t_done", "t_split", "tt_done", "tt_ok"))
        g_done, g_free, g_ok, g_out = map(sem, ("g_done", "g_free", "g_ok", "g_out"))
        gs_first = sem("gs_first")
        gs_in = [sem(f"gs_in{c}") for c in range(OUTS // TILE)]
        tile_done, acc_free = map(sem, ("tile_done", "acc_free"))
        first_kept = sem("first_kept")
        kept = [sem("kept0"), sem("kept1")]
        back_in = [sem("back_in0"), sem("back_in1")]
        out_free = [sem("out_free0"), sem("out_free1")]

        SETUP_GROUPS = GROUPS * (1 + FIRST + 1 + ROWS)
        NB = BATCHES // 2

        first_steps = [(1, "b_abs", 0), (3.5, "b_scale", 0), (4, "b_turn", 0), (8, "b_lo", 0), (8.5, "b_out", 0),
                       (9.5, "a_abs", 0), (10, "a_sum", 0), (12.5, "a_scale", 0), (13, "a_spread", 0),
                       (14.5, "a_scaled", 0), (16.5, "a_hi", 0), (20.5, "a_lo", 0), (22, "a_out", 0)]
        for r in range(ROWS):
            end = (r + 1) * PIECES
            first_steps += [(r * PIECES + n, "terms", (r, n)) for n in range(0, PIECES, 2)]
            first_steps += [(end + 0.5, "v_abs", r), (end + 3, "v_scale", r), (end + 3.1, "v_turn", r),
                            (end + 7.5, "v_lo", r), (end + 8, "v_spread", r), (end + 8.2, "v_rows", r)]
        for q in range(FIRST + 1):
            at = 9 + 8 * q if q < FIRST else 152
            first_steps += [(at, "x_abs", q), (at + 2.5, "x_scale", q), (at + 3, "x_turn", q),
                            (at + 7.5, "x_lo", q)]
            if q < FIRST:
                first_steps += [(at + 8, "t", q), (at + 10, "t_parts", q), (at + 11, "tt", q)]
        first_steps += [(130 + 2 * q, "keep", q) for q in range(FIRST)]
        for step in range(STEPS):
            end = 2 * (step + 1) * PIECES
            first_steps += [(end + 8.9, "g", step), (end + 14, "g_parts", step), (end + 15, "g_store", step)]
        for n in range(STEPS * FIRST):
            first_steps += [(49 + 4 * n, "tile", n), (49 + 4 * n + 5, "evacuate", n)]
        first_steps = [(kind, i) for _, kind, i in sorted(first_steps, key=lambda s: s[0])]
        first_group, count = {}, 0
        for kind, i in first_steps:
            if kind in ("b_turn", "x_turn", "v_turn"):
                first_group[kind, i] = count
                count += GROUPS
        assert count == SETUP_GROUPS

        class Phase:
            def __init__(self, first, batches, chunks, before, rows):
                self.first, self.batches, self.chunks, self.rows = first, batches, chunks, rows
                self.c = len(chunks)
                if self.c == 2:
                    self.at = {(0, 12): "x", (1, 2): "x", (1, 6): "x", (1, 10): "x"}
                else:
                    self.at = {(1, 4): "x", (1, 12): "x", (2, 4): "x", (2, 12): "x"}
                self.tiles = PER_BATCH * self.c
                self.groups = PER_BATCH * GROUPS + rows * GROUPS
                self.q0, self.n0, self.g0, self.s0, self.l0 = before

            def after(self):
                return (self.q0 + self.batches * PER_BATCH, self.n0 + self.batches * self.tiles,
                        self.g0 + self.batches * self.groups, self.s0 + self.batches,
                        [n + self.batches * (c in self.chunks) for c, n in enumerate(self.l0)])

            def jobs(self, j, ci):
                at = dict(self.at)
                if self.rows and j % 2 == 1:
                    at = {(0, 12): "x", (1, 1): "x", (1, 3): "v", (1, 5): "v", (1, 6): "x", (1, 8): "v",
                          (1, 10): "x", (1, 12): "v"}
                found = []
                per_block = [self.per_block(i) for i in range(j)]
                base = sum(per_block)
                order = sorted(at.items())
                seen = {"x": 0, "v": 0}
                for n, ((c, k), kind) in enumerate(order):
                    if c == ci:
                        found.append((k, kind, seen[kind], base + n))
                    seen[kind] += 1
                return found

            def free_for_row(self, i):
                last = [g for j in range(2 * i) for ci in range(self.c) for _, kind, _, g in self.jobs(j, ci)
                        if kind == "v"]
                if i == 0:
                    return self.free_for_row(2) - self.groups
                return max(last) + 1

            def per_block(self, j):
                return GROUPS * (2 if self.rows and j % 2 == 1 else 1)

        FB = FIRST // PER_BATCH
        p2 = Phase(FB, NB, (0, 1), (FIRST, STEPS * FIRST, SETUP_GROUPS, FB, [0] * len(gs_in)), 2)
        p3 = Phase(FB + NB, BATCHES - FB - NB, (0, 1, 2, 3), p2.after(), 0)
        p4 = Phase(0, FB + NB, (2, 3), p3.after(), 0)
        assert NB * p2.rows == ROWS

        block = ctx.enter_context(nc.Block())

        def group_view(bank):
            return bank[:].rearrange("p (m c) -> p m c", m=GROUP)

        def store_g(eng, piece):
            eng.wait_ge(g_ok, piece + 1)
            for dup in range(2):
                for part, src in enumerate((g_hi, g_lo)):
                    r0 = (2 * part + dup) * RANK
                    eng.dma_start(g_dram[:, r0:r0 + RANK, piece * GP:(piece + 1) * GP],
                                  src[:].bitcast(F32)).then_inc(g_out, 16)

        def first_tile(n):
            return n // FIRST, n % FIRST

        @block.sync
        def _(sp):
            AHEAD = 10

            def load_wq(r, pieces):
                for n in pieces:
                    a, h = n // 2, n % 2
                    if not (isinstance(r, int) and r * PIECES + n < WQ_SLOTS):
                        sp.wait_ge(wq_used, r * PIECES + n - WQ_SLOTS + 1)
                    sp.dma_start(wq_sb[:, n % WQ_SLOTS, :],
                                 wq_v[a, bass.ds(r, 1), :, h * PIECE:(h + 1) * PIECE].rearrange(
                                     "r p i -> (r p) i")).then_inc(wq_in[n % WQ_SLOTS], 16)

            def load_weight(r, v, free):
                if free is not None:
                    sp.wait_ge(tr_done, free)
                sp.dma_start(v, w_v[bass.ds(r, 1)].rearrange("r p i -> (r p) i")).then_inc(w_in, 16)

            load_weight(0, v_nat[:], None)
            load_wq(0, range(WQ_SLOTS))
            sp.dma_start(ids_sb[:], ids.rearrange("(a b) -> a b", a=1)).then_inc(ids_in, 16)
            sp.wait_ge(ids_in, 16)
            for b in range(BATCHES):
                n = sp.value_load(ids_sb[0:1, b:b + 1], min_val=0, max_val=lora_a.shape[0] - 1)
                sp.dma_start(b_nat[b * RANK:(b + 1) * RANK, :],
                             lora_b[bass.ds(n, 1)].rearrange("n r i -> (n r) i")).then_inc(b_in, 16)
                sp.dma_start(a_nat[:, :, b * RANK:(b + 1) * RANK],
                             a_v[bass.ds(n, 1)].rearrange("n p k r -> (n p) k r")).then_inc(a_in, 16)
            for r in range(ROWS):
                load_wq(r, range(WQ_SLOTS if r == 0 else 0, AHEAD))
                if r < ROWS - 1:
                    load_weight(r + 1, v_nat[:] if r % 2 else v_other,
                                first_group["v_turn", r - 1] + GROUPS if r else None)
                load_wq(r, range(AHEAD, PIECES))
            with sp.Fori(0, p2.batches) as it:
                for i in range(2):
                    r = ROWS + it * 2 + i
                    load_wq(r, range(WQ_SLOTS))
                    load_weight(r, v_nat[:], p2.g0 + it * p2.groups + p2.free_for_row(i))
                    load_wq(r, range(WQ_SLOTS, PIECES))
            sp.wait_ge(wq_used, 2 * ROWS * PIECES)
            sp.dma_start(wq_sb[:].rearrange("p s c -> p (s c)").bitcast(F16)[:, 0:2 * D],
                         a_dram).then_inc(a_back, 16)
            for piece in range(STEPS, 2 * STEPS):
                store_g(sp, piece)
            sp.wait_ge(g_out, 16 * 4 * OUTS // GP)
            for slot in range(2):
                sp.wait_ge(kept[slot], 32 * (1 + p2.batches * PER_BATCH // 2))
            with sp.Fori(0, p4.batches) as it:
                for j in range(PER_BATCH):
                    sp.wait_ge(tile_done, p4.n0 + it * p4.tiles + (j - 1) * p4.c + 1)
                    blk = bass.ds((it + p4.first) * PER_BATCH + j, 1)
                    sp.dma_start(xt[:, j % 2].rearrange("p s k c -> p (s k c)"),
                                 xt_dram[blk].rearrange("b p c -> (b p) c")).then_inc(back_in[j % 2], 16)
                    sp.dma_start(t_t[:, j % 2, :].bitcast(F32),
                                 tt_dram[blk].rearrange("b p c -> (b p) c")).then_inc(back_in[j % 2], 16)

        @block.gpsimd
        def _(pool):
            pool.memset(ones[:], 1.0).then_inc(tile_done, 1)
            pool.memset(ident[:], 0.0).then_inc(ident_ok, 1)
            pool.wait_ge(ident_ok, 1)
            pool.affine_select(out=ident[:], in_=ident[:], compare_op=ALU.not_equal, fill=1.0, base=0,
                               pattern=[[-1, P]], channel_multiplier=1).then_inc(ident_ok, 1)

            bt_flat = bt[:].rearrange("p k c -> p (k c)")

            def load_bt(b):
                pool.dma_start(bt_flat, bt_dram[bass.ds(b, 1)].rearrange("b p c -> (b p) c")).then_inc(bt_in, 16)

            pool.wait_ge(bt_out, 16)
            load_bt(0)
            pool.wait_ge(t_done, PER_BATCH)
            load_bt(1)

            def load_first_stacks(step):
                cols = slice(step * GP, (step + 1) * GP)
                pool.wait_ge(g_out, 16 * 4 * (step + 1))
                pool.wait_ge(gb_out, 16 * 2 * (step + 1))
                for b in range(FB):
                    to = slice(b * HALF + step * GP, b * HALF + (step + 1) * GP)
                    pool.dma_start(g_st[0:4 * RANK, to].bitcast(F32), g_dram[b, :, cols]).then_inc(gs_first, 16)
                    pool.dma_start(g_st[4 * RANK:STACK, to].bitcast(F32), gb_dram[:, cols]).then_inc(gs_first, 16)

            load_first_stacks(0)
            for n in range(STEPS * FIRST):
                step, q = first_tile(n)
                if n == PER_BATCH:
                    pool.wait_ge(t_done, 2 * PER_BATCH)
                    load_bt(2)
                if q == FIRST - 2 and step < STEPS - 1:
                    load_first_stacks(step + 1)
                pool.wait_ge(acc_free, n + ACC_BANKS + 1)
                pool.dma_start(out_v[q, :, step * GP:(step + 1) * GP], out_sb[:, n % 2, 0:GP]
                               ).then_inc(out_free[n % 2], 16)

            def stacks_ready(ph):
                pool.wait_ge(g_out, 16 * 4 * ((ph.chunks[-1] + 1) * TILE // GP))
                pool.wait_ge(gb_out, 16 * (ph.chunks[-1] + 1) * TILE // P)

            def batch(ph, it, more):
                b = it + ph.first
                n = ph.n0 + it * ph.tiles
                pool.wait_ge(tile_done, n + 1)
                for c in ph.chunks:
                    cols = slice(c * TILE, (c + 1) * TILE)
                    pool.dma_start(g_st[0:4 * RANK, cols].bitcast(F32),
                                   g_dram[bass.ds(b, 1), :, cols].rearrange("b r o -> (b r) o")
                                   ).then_inc(gs_in[c], 16)
                    pool.dma_start(g_st[4 * RANK:STACK, cols].bitcast(F32), gb_dram[:, cols]
                                   ).then_inc(gs_in[c], 16)
                for j in range(PER_BATCH):
                    for ci, c in enumerate(ph.chunks):
                        t = j * ph.c + ci
                        pool.wait_ge(acc_free, n + t + ACC_BANKS + 1)
                        pool.dma_start(
                            out_v[bass.ds(b * PER_BATCH + j, 1), :, c * TILE:(c + 1) * TILE].rearrange(
                                "t p o -> (t p) o"), out_sb[:, t % 2, :]).then_inc(out_free[t % 2], 16)
                        if j == PER_BATCH - 1 and ci == 0 and more:
                            pool.wait_ge(t_done, ph.q0 + it * PER_BATCH + PER_BATCH)
                            load_bt(b + 1)

            stacks_ready(p2)
            with pool.Fori(0, p2.batches) as it:
                batch(p2, it, True)
            stacks_ready(p3)
            for it in range(p3.batches):
                batch(p3, it, it < p3.batches - 1)
            with pool.Fori(0, p4.batches) as it:
                batch(p4, it, False)
            last = p4.after()[1]
            for s in range(2):
                pool.wait_ge(out_free[s], 16 * (last // 2))

        @block.scalar
        def _(act):
            def load_x(blk):
                act.dma_start(x_nat[:], x_v[bass.ds(blk, 1)].rearrange("t p i -> (t p) i")).then_inc(x_in, 16)

            def load_first_x(q):
                done = x_in_other if q in X_OTHER else x_in
                act.dma_start(x_places[q], x_v[q]).then_inc(done, 16)

            def abs_sums(src, col, done):
                for h in range(2):
                    if h:
                        act.drain()
                    s = act.activation(junk[:], src[:, h * PIECE:(h + 1) * PIECE], ACT.Abs,
                                       bias=c0[:] if done is v_abs else 0.0,
                                       accum_out=sums[:, col + h:col + h + 1])
                s.then_inc(done, 1)

            def hi(g, bank, dst):
                act.wait_ge(tr_done, g + 1)
                act.activation(dst, group_view(tr[bank]), ACT.Copy).then_inc(hi_done, 1)

            def v_abs_sums(r, v):
                act.drain()
                act.wait_ge(v_sum, r + 1)
                abs_sums(v, 2, v_abs)

            def v_to_scale(r, v):
                act.wait_ge(v_scale, r + 1)
                act.activation(v, v, ACT.Identity, bias=v_sc[:, 2:3],
                               scale=v_sc[:, 0:1]).then_inc(v_scaled, 1)

            def v_hi(half, r, m, g, bank):
                o = (r - half * ROWS) * P
                hi(g, bank, vt[half][:, 0, m * GROUP:(m + 1) * GROUP, bass.ds(o, P)])

            def v_rows(r, first=False):
                act.wait_ge(v_bc, r + 1)
                act.activation(v_inv[:, bass.ds(r * P, P)], inv_ps, ACT.Copy)
                if not first:
                    act.wait_ge(gb_out, 16 * r)
                act.activation(b_row[:], brow_ps, ACT.Copy).then_inc(v_row, 1)
                act.wait_ge(v_row, r + 1)
                act.dma_start(gb_dram[:, bass.ds(r * P, P)], b_row[:].bitcast(F32)).then_inc(gb_out, 16)

            def x_abs_sums(q, place=x_nat[:]):
                act.drain()
                if isinstance(q, int) and q in X_OTHER:
                    act.wait_ge(x_in_other, 16 * (X_OTHER.index(q) + 1))
                elif isinstance(q, int) and q < FIRST:
                    act.wait_ge(x_in, 16 * (q + 1 - sum(other < q for other in X_OTHER)))
                else:
                    act.wait_ge(x_in, 16 * (q + 1 - len(X_OTHER)))
                abs_sums(place, 0, x_abs)

            def x_to_scale(q, scale_slot, place=x_nat[:]):
                act.wait_ge(x_scale, q + 1)
                act.activation(place, place, ACT.Copy, scale=x_sc[:, scale_slot, 0:1]).then_inc(x_scaled, 1)

            def x_hi(dst, m, g, bank):
                hi(g, bank, dst[:, 0, m * GROUP:(m + 1) * GROUP, :])

            def tt_copy(q, slot):
                act.wait_ge(tt_done, q + 1)
                act.activation(t_t[:, slot, :], tt_ps, ACT.Copy).then_inc(tt_ok, 1)

            def keep(blk, x_t, slot, done):
                act.dma_start(xt_dram[blk].rearrange("b p c -> (b p) c"),
                              x_t.rearrange("p s k c -> p (s k c)")).then_inc(done, 16)
                act.dma_start(tt_dram[blk].rearrange("b p c -> (b p) c"),
                              t_t[:, slot, :].bitcast(F32)).then_inc(done, 16)

            for i, src in enumerate((scale, wscale, bscale)):
                act.dma_start(small[:, i, :], src.rearrange("(o a) -> o a", o=1).to_broadcast([P, ADAPTERS])
                              ).then_inc(small_in, 16)
            act.dma_start(zp_i[:], zp.rearrange("(o a) -> o a", o=1).to_broadcast([P, ADAPTERS])).then_inc(small_in, 16)
            act.dma_start(bq_i[:], bq.rearrange("a (r p) -> (a r) p", p=P)).then_inc(small_in, 16)
            act.dma_start(bias_rows[:], bias.rearrange("(r p) -> r p", p=P)).then_inc(small_in, 16)
            load_first_x(0)
            load_first_x(1)

            for kind, i in first_steps:
                g = first_group.get((kind, i))
                if kind == "b_abs":
                    act.wait_ge(b_in, 16 * BATCHES)
                    abs_sums(b_nat, 4, b_abs)
                elif kind == "b_turn":
                    act.wait_ge(b_scale, 1)
                    act.activation(b_nat, b_nat, ACT.Copy, scale=b_sc[:, 0:1]).then_inc(b_scaled, 1)
                    for m in range(GROUPS):
                        act.wait_ge(tr_done, g + m + 1)
                        act.activation(
                            bt_all[:, :, m * GROUP:(m + 1) * GROUP, RANK:].rearrange("p b k r -> p k b r"),
                            tr[m][:].rearrange("p (k b r) -> p k b r", k=GROUP, b=BATCHES),
                            ACT.Copy).then_inc(hi_done, 1)
                elif kind == "b_out":
                    act.wait_ge(tr_free, TR_BANKS + first_group["b_turn", 0] + GROUPS)
                    act.dma_start(bt_dram.rearrange("b p c -> p b c"),
                                  bt_all.rearrange("p b k c -> p b (k c)")).then_inc(bt_out, 16)
                elif kind == "a_abs":
                    act.wait_ge(a_in, 16 * BATCHES)
                    act.activation(a_abs, a_nat, ACT.Abs).then_inc(a_absd, 1)
                elif kind == "a_hi":
                    act.wait_ge(a_scaled, 1)
                    act.activation(a_first[:, 0], a_nat, ACT.Copy).then_inc(a_hi, 1)
                elif kind == "a_out":
                    act.wait_ge(a_hi, 1)
                    act.wait_ge(a_lo, 1)
                    act.dma_start(a_dram, half1[:, 14 * D:16 * D]).then_inc(a_out, 16)
                elif kind == "x_abs":
                    x_abs_sums(i, x_places[i])
                elif kind == "x_turn":
                    x_to_scale(i, i % FIRST, x_places[i])
                    if i == 4:
                        act.wait_ge(bt_out, 16)
                    if i == FIRST:
                        act.wait_ge(kept[0], 32)
                    for m in range(GROUPS):
                        x_hi(xt_first[i % FIRST], m, g + m, (g + m) % TR_BANKS)
                    if i + 2 < FIRST - 1:
                        if i + 2 == X_OTHER[1]:
                            act.wait_ge(a_lo, 1)
                        load_first_x(i + 2)
                    elif i >= FIRST - 2:
                        load_x(i + 1)
                elif kind == "tt":
                    tt_copy(i, i)
                elif kind == "v_abs":
                    v_abs_sums(i, v_other if i % 2 else v_nat[:])
                elif kind == "v_turn":
                    v_to_scale(i, v_other if i % 2 else v_nat[:])
                    for m in range(GROUPS):
                        v_hi(0, i, m, g + m, (g + m) % TR_BANKS)
                elif kind == "v_rows":
                    v_rows(i, i == 0)
                elif kind == "g_store":
                    store_g(act, i)
                elif kind == "keep":
                    act.wait_ge(tt_ok, i + 1)
                    keep(slice(i, i + 1), xt_first[i], i, kept[i] if i < 2 else first_kept)
            act.wait_ge(first_kept, 32 * (FIRST - 2))
            act.wait_ge(a_out, 16)

            def batch(ph, it, last=False):
                q0, g0 = ph.q0 + it * PER_BATCH, ph.g0 + it * ph.groups
                for j in range(PER_BATCH):
                    q = q0 + j
                    for ci in range(ph.c):
                        more = not (last and j == PER_BATCH - 1)
                        if ci == 0:
                            if more:
                                x_abs_sums(q + 1)
                                x_to_scale(q + 1, (j + 1) % 2)
                            if ph is p2:
                                act.wait_ge(kept[j % 2], 32 * (1 + it * 2 + j // 2))
                            tt_copy(q, j % 2)
                            if ph is p2:
                                act.wait_ge(tt_ok, q + 1)
                                keep(bass.ds(q, 1), xt[:, j % 2], j % 2, kept[j % 2])
                        r = ROWS + it * 2 + j // 2
                        if ph.rows and j % 2 == 1 and ci == 0:
                            v_abs_sums(r, v_nat[:])
                            v_to_scale(r, v_nat[:])
                        for k, kind, m, g in ph.jobs(j, ci):
                            if kind == "x" and more:
                                if ph is p2 and m == 0:
                                    act.wait_ge(kept[(j + 1) % 2], 32 * (1 + it * 2 + (j + 1) // 2))
                                x_hi(xt[:, (j + 1) % 2], m, g0 + g, g % TR_BANKS)
                                if m == GROUPS - 1 and not (last and j == PER_BATCH - 2):
                                    load_x(q + 2)
                            elif kind == "v":
                                v_hi(1, r, m, g0 + g, g % TR_BANKS)
                        if ph.rows and j % 2 == 1 and ci == 1:
                            v_rows(r)

            with act.Fori(0, p2.batches) as it:
                batch(p2, it)
            for slot in range(2):
                act.wait_ge(kept[slot], 32 * (1 + p2.batches * PER_BATCH // 2))
            for it in range(p3.batches):
                batch(p3, it, it == p3.batches - 1)

        @block.vector
        def _(dve):
            def pow2(total, s, inv):
                ti, bi = total.bitcast(I32), bits[:].bitcast(I32)
                dve.drain()
                dve.tensor_scalar(bi, ti, EXP_MASK, None, ALU.bitwise_and)
                dve.drain()
                dve.tensor_scalar(bi, bi, -1.0, SCALE_BITS, ALU.mult, ALU.add)
                dve.drain()
                dve.tensor_scalar(s.bitcast(I32), bi, MAX_BITS, MIN_BITS, ALU.min, ALU.max)
                dve.drain()
                return dve.tensor_scalar(inv.bitcast(I32), s.bitcast(I32), -1.0, INV_BITS, ALU.mult, ALU.add)

            def lo(g, bank, dst, part_hi):
                dve.wait_ge(hi_done, g + 1)
                dve.tensor_tensor(dst, group_view(tr[bank]), part_hi, ALU.subtract).then_inc(tr_free, 1)

            def x_pow2(q, slot):
                dve.wait_ge(x_abs, q + 1)
                dve.tensor_tensor(tot[:], sums[:, 0:1], sums[:, 1:2], ALU.add)
                pow2(tot[:], x_sc[:, slot, 0:1], x_sc[:, slot, 1:2]).then_inc(x_scale, 1)

            def x_lo(dst, m, g, bank):
                ks = slice(m * GROUP, (m + 1) * GROUP)
                lo(g, bank, dst[:, 1, ks, :], dst[:, 0, ks, :])

            def v_terms(r, pieces, v=v_nat[:]):
                for n in pieces:
                    a, h = n // 2, n % 2
                    if n == 0:
                        dve.wait_ge(w_in, 16 * (r + 1))
                    dve.wait_ge(wq_in[n % WQ_SLOTS], 16 * (r * (PIECES // WQ_SLOTS) + n // WQ_SLOTS + 1))
                    if n >= 2:
                        dve.wait_ge(wq_used, r * PIECES + n - 1)
                    dst = v[:, h * PIECE:(h + 1) * PIECE]
                    dve.scalar_tensor_tensor(dst, wq_sb[:, n % WQ_SLOTS, :], coef[:, 0, a:a + 1], dst,
                                             ALU.mult, ALU.add).then_inc(wq_used, 1)
                if n == PIECES - 1:
                    dve.wait_ge(wq_used, (r + 1) * PIECES)
                    own = v[:, bass.ds(r * P, P)]
                    dve.tensor_tensor(own, own, ident[:], ALU.add).then_inc(v_sum, 1)

            def v_pow2(r):
                dve.wait_ge(v_abs, r + 1)
                dve.tensor_tensor(tot[:], sums[:, 2:3], sums[:, 3:4], ALU.add)
                pow2(tot[:], v_sc[:, 0:1], v_sc[:, 1:2])
                dve.drain()
                dve.tensor_scalar(v_sc[:, 2:3], c0[:], v_sc[:, 0:1], None, ALU.mult).then_inc(v_scale, 1)
                dve.tensor_scalar(diag[:], ident[:], v_sc[:, 1:2], None, ALU.mult)
                dve.tensor_scalar(b_tmp[:], b_col[:, bass.ds(r, 1)], v_sc[:, 0:1], None, ALU.mult)
                dve.drain()
                dve.tensor_copy(b_pair[:, 0:1], b_tmp[:])
                dve.drain()
                dve.tensor_tensor(b_pair[:, 1:2], b_tmp[:], b_pair[:, 0:1].bitcast(F32),
                                  ALU.subtract).then_inc(v_diag, 1)

            def v_lo(half, r, m, g, bank):
                o = (r - half * ROWS) * P
                ks = slice(m * GROUP, (m + 1) * GROUP)
                lo(g, bank, vt[half][:, 1, ks, bass.ds(o, P)], vt[half][:, 0, ks, bass.ds(o, P)])

            def t_parts(q, slot):
                dve.wait_ge(t_done, q + 1)
                dve.tensor_copy(t_lo[:], t_ps[:, 0:RANK])
                dve.drain()
                dve.tensor_tensor(t_f[:], t_ps[:, RANK:2 * RANK], t_lo[:], ALU.add)
                dve.drain()
                parts = t_st[:, 0:4 * RANK].rearrange("p (u s r) -> p u s r", u=2, s=2)
                twice = t_f[:].rearrange("p (u r) -> p u r", u=1).to_broadcast([P, 2, RANK])
                dve.tensor_copy(parts[:, :, 0, :], twice)
                dve.tensor_copy(t_st[:, 4 * RANK:STACK], x_sc[:, slot, 0:1].to_broadcast([P, 2]))
                dve.drain()
                dve.tensor_tensor(parts[:, :, 1, :], twice, parts[:, :, 0, :].bitcast(F32),
                                  ALU.subtract).then_inc(t_split, 1)

            def evacuate(n, pair, parity, slot, cols):
                dve.wait_ge(tile_done, n + 2)
                if not (isinstance(pair, int) and pair == 0):
                    dve.wait_ge(out_free[parity], 16 * pair)
                size = cols.stop - cols.start
                dve.scalar_tensor_tensor(out_sb[:, parity, 0:size], acc[parity][:, 0:size],
                                         x_sc[:, slot, 1:2], v_inv[:, cols], ALU.mult, ALU.mult
                                         ).then_inc(acc_free, 1)

            def g_parts(pieces):
                for n in pieces:
                    at, done = (0, n + 1) if n < STEPS else (n % 2 * GP, STEPS + (n - STEPS) // 2 + 1)
                    dve.wait_ge(g_done, done)
                    if n:
                        dve.wait_ge(g_out, 16 * 4 * n)
                    dve.tensor_scalar(g_f[:], g_ps[:, at:at + GP], a_sc[:, 1:2], b_sc[:, 1:2],
                                      ALU.mult, ALU.mult).then_inc(g_free, 1)
                    dve.drain()
                    dve.tensor_copy(g_hi[:], g_f[:])
                    dve.drain()
                    dve.tensor_tensor(g_lo[:], g_f[:], g_hi[:].bitcast(F32), ALU.subtract).then_inc(g_ok, 1)

            dve.memset(tot[:], 0.0).then_inc(tr_free, TR_BANKS)
            dve.memset(bits[:], 0.0).then_inc(acc_free, ACC_BANKS)
            dve.wait_ge(small_in, 16 * 6)
            dve.tensor_copy(small[:, 3, :], zp_i[:])
            dve.tensor_copy(bq_f[:], bq_i[:]).then_inc(bq_ok, 1)
            dve.tensor_tensor(coef[:, 0, :], small[:, 0, :], small[:, 1, :], ALU.mult)
            dve.tensor_tensor(coef[:, 1, :], small[:, 0, :], small[:, 2, :], ALU.mult)
            dve.drain()
            dve.tensor_tensor(zprod[:], small[:, 0, :], small[:, 3, :], ALU.mult)
            dve.drain()
            dve.tensor_reduce(c0[:], zprod[:], AX.X, ALU.add)
            dve.drain()
            dve.wait_ge(bqt_ok, 1)
            dve.tensor_scalar(b_col[:], bias_ps, c0[:], None, ALU.add)
            for a in range(ADAPTERS):
                dve.drain()
                dve.scalar_tensor_tensor(b_col[:], bq_ps[:, a * KB:(a + 1) * KB], coef[:, 1, a:a + 1], b_col[:],
                                         ALU.mult, ALU.add)
            dve.drain()

            for kind, i in first_steps:
                g = first_group.get((kind.split("_")[0] + "_turn", i))
                if kind == "b_scale":
                    dve.wait_ge(b_abs, 1)
                    dve.tensor_tensor(tot[:], sums[:, 4:5], sums[:, 5:6], ALU.add)
                    pow2(tot[:], b_sc[:, 0:1], b_sc[:, 1:2]).then_inc(b_scale, 1)
                elif kind == "b_lo":
                    for m in range(GROUPS):
                        ks = slice(m * GROUP, (m + 1) * GROUP)
                        dve.wait_ge(hi_done, g + m + 1)
                        dve.tensor_tensor(bt_all[:, :, ks, 0:RANK].rearrange("p b k r -> p k b r"),
                                          tr[m][:].rearrange("p (k b r) -> p k b r", k=GROUP, b=BATCHES),
                                          bt_all[:, :, ks, RANK:].rearrange("p b k r -> p k b r"),
                                          ALU.subtract).then_inc(tr_free, 1)
                elif kind == "a_scale":
                    dve.wait_ge(a_sum, 1)
                    dve.tensor_copy(sums[:, 6:7], asum_ps)
                    pow2(sums[:, 6:7], a_sc[:, 0:1], a_sc[:, 1:2])
                    dve.drain()
                    dve.tensor_scalar(diag[:], ident[:], a_sc[:, 0:1], None, ALU.mult).then_inc(a_diag, 1)
                elif kind == "a_scaled":
                    dve.wait_ge(a_bc, 1)
                    spread = abc_ps.rearrange("p (k c) -> p k c", k=1).to_broadcast([P, KB, P])
                    dve.tensor_tensor(a_nat, a_nat, spread, ALU.mult).then_inc(a_scaled, 1)
                elif kind == "a_lo":
                    dve.wait_ge(a_hi, 1)
                    dve.tensor_tensor(a_first[:, 1], a_nat, a_first[:, 0], ALU.subtract).then_inc(a_lo, 1)
                elif kind == "terms":
                    r, n = i
                    v_terms(r, (n, n + 1), v_other if r % 2 else v_nat[:])
                elif kind == "v_scale":
                    v_pow2(i)
                elif kind == "v_lo":
                    for m in range(GROUPS):
                        v_lo(0, i, m, g + m, (g + m) % TR_BANKS)
                elif kind == "x_scale":
                    x_pow2(i, i % FIRST)
                    if i < FIRST:
                        dve.wait_ge(x_scale, i + 1)
                        dve.tensor_copy(x_inv[:, i:i + 1], x_sc[:, i, 1:2])
                elif kind == "x_lo":
                    for m in range(GROUPS):
                        x_lo(xt_first[i % FIRST], m, g + m, (g + m) % TR_BANKS)
                elif kind == "t_parts":
                    t_parts(i, i)
                elif kind == "g_parts":
                    g_parts((i,))
                elif kind == "evacuate":
                    step, q = first_tile(i)
                    evacuate(i, i // 2, i % 2, q, slice(step * GP, (step + 1) * GP))

            def tile_out(ph, it, t, c, slot):
                evacuate(ph.n0 + it * ph.tiles + t, ph.n0 // 2 + it * (ph.tiles // 2) + t // 2, t % 2,
                         slot, slice(c * TILE, (c + 1) * TILE))

            def batch(ph, it, last=False):
                q0, g0 = ph.q0 + it * PER_BATCH, ph.g0 + it * ph.groups
                for j in range(PER_BATCH):
                    more = not (last and j == PER_BATCH - 1)
                    for ci, c in enumerate(ph.chunks):
                        t = j * ph.c + ci
                        if t:
                            tile_out(ph, it, t - 1, ph.chunks[(ci - 1) % ph.c], (j - (ci == 0)) % 2)
                        if ci == 0:
                            t_parts(q0 + j, j % 2)
                            if ph is p2:
                                dve.tensor_copy(x_inv[:, bass.ds(q0 + j, 1)], x_sc[:, j % 2, 1:2])
                            if more:
                                x_pow2(q0 + j + 1, (j + 1) % 2)
                        r = ROWS + it * 2 + j // 2
                        if ph.rows:
                            share = (range(0, 6), range(6, 12), range(12, PIECES), ())[(j % 2) * 2 + ci]
                            if len(share):
                                v_terms(r, share)
                        if ph.rows and (j % 2) * 2 + ci == 2:
                            v_pow2(r)
                        for k, kind, m, g in ph.jobs(j, ci):
                            if kind == "x" and more:
                                x_lo(xt[:, (j + 1) % 2], m, g0 + g, g % TR_BANKS)
                            elif kind == "v":
                                v_lo(1, r, m, g0 + g, g % TR_BANKS)
                tile_out(ph, it, ph.tiles - 1, ph.chunks[-1], (PER_BATCH - 1) % 2)

            def batch_again(ph, it):
                for j in range(PER_BATCH):
                    dve.tensor_copy(x_sc[:, j % 2, 1:2], x_inv[:, bass.ds((it + ph.first) * PER_BATCH + j, 1)])
                    dve.drain()
                    for ci, c in enumerate(ph.chunks):
                        tile_out(ph, it, j * ph.c + ci, c, j % 2)

            with dve.Fori(0, p2.batches) as it:
                batch(p2, it)
            g_parts(range(STEPS, 2 * STEPS))
            for it in range(p3.batches):
                batch(p3, it, it == p3.batches - 1)
            with dve.Fori(0, p4.batches) as it:
                batch_again(p4, it)

        @block.tensor
        def _(pe):
            def group(g, bank, src, m):
                pe.wait_ge(tr_free, g + 1)
                for i in range(GROUP):
                    k = m * GROUP + i
                    last = pe.transpose(tr[bank][:, i * P:(i + 1) * P], src[:, k * P:(k + 1) * P], ident[:])
                last.then_inc(tr_done, 1)

            def v_spread(r, pieces):
                if pieces:
                    pe.wait_ge(g_free, pieces)
                pe.wait_ge(v_diag, r + 1)
                pe.matmul(inv_ps, ones[:], diag[:], start=True, stop=True)
                pe.transpose(brow_ps, b_pair[:].bitcast(F32), ident[:]).then_inc(v_bc, 1)

            def g_product(a_parts, v, size, done, rows, groups):
                pe.wait_ge(v_row, rows)
                pe.wait_ge(tr_free, TR_BANKS + groups)
                if done:
                    pe.wait_ge(g_free, done)
                for k in range(KB):
                    for s, (pa, pv) in enumerate(((0, 0), (0, 1), (1, 0))):
                        last = pe.matmul(g_ps[:, 0:size], a_parts[:, pa, k, :], v[:, pv, k, :],
                                         start=(k == 0 and s == 0), stop=(k == KB - 1 and s == 2))
                last.then_inc(g_done, 1)

            def t_product(q, x_t, groups):
                pe.wait_ge(tr_free, TR_BANKS + groups)
                if not (isinstance(q, int) and q == 0):
                    pe.wait_ge(tt_ok, q)
                for k in range(KB):
                    pe.matmul(t_ps, x_t[:, 0, k, :], bt[:, k, :], start=(k == 0), stop=False)
                    last = pe.matmul(t_ps[:, RANK:], x_t[:, 1, k, :], bt[:, k, RANK:],
                                     start=False, stop=(k == KB - 1))
                last.then_inc(t_done, 1)

            def tt_turn(q):
                pe.wait_ge(t_split, q + 1)
                pe.transpose(tt_ps, t_st[:].bitcast(F32), ident[:]).then_inc(tt_done, 1)

            pe.wait_ge(ident_ok, 2)
            pe.wait_ge(bq_ok, 1)
            pe.transpose(bq_ps, bq_f[:], ident[:])
            pe.transpose(bias_ps, bias_rows[:], ident[0:OUTS // P, 0:OUTS // P]).then_inc(bqt_ok, 1)

            for kind, i in first_steps:
                g = first_group.get((kind, i))
                if kind == "b_turn":
                    pe.wait_ge(b_scaled, 1)
                    for m in range(GROUPS):
                        group(g + m, (g + m) % TR_BANKS, b_nat, m)
                elif kind == "a_sum":
                    pe.wait_ge(a_absd, 1)
                    for k in range(KB):
                        last = pe.matmul(asum_ps, a_abs[:, k, :], ones[:, 0:1], start=(k == 0), stop=(k == KB - 1))
                    last.then_inc(a_sum, 1)
                elif kind == "a_spread":
                    pe.wait_ge(a_diag, 1)
                    pe.matmul(abc_ps, ones[:], diag[:], start=True, stop=True).then_inc(a_bc, 1)
                elif kind == "x_turn":
                    pe.wait_ge(x_scaled, i + 1)
                    for m in range(GROUPS):
                        group(g + m, (g + m) % TR_BANKS, x_places[i], m)
                elif kind == "t":
                    pe.wait_ge(bt_in, 16 * (i // PER_BATCH + 1))
                    t_product(i, xt_first[i], first_group["x_turn", i] + GROUPS)
                elif kind == "tt":
                    tt_turn(i)
                elif kind == "v_turn":
                    pe.wait_ge(v_scaled, i + 1)
                    for m in range(GROUPS):
                        group(g + m, (g + m) % TR_BANKS, v_other if i % 2 else v_nat, m)
                elif kind == "v_spread":
                    v_spread(i, i // 2)
                elif kind == "g":
                    if i == 0:
                        pe.wait_ge(a_lo, 1)
                    g_product(a_first, vt0[:, :, :, i * GP:(i + 1) * GP], GP, i, 2 * i + 2,
                              first_group["v_turn", 2 * i + 1] + GROUPS)
                elif kind == "tile":
                    step, q = first_tile(i)
                    bank = acc[i % ACC_BANKS][:, 0:GP]
                    pe.wait_ge(acc_free, i + 1)
                    for k in range(KB):
                        for s, (px, pv) in enumerate(((0, 0), (0, 1), (1, 0))):
                            pe.matmul(bank, xt_first[q][:, px, k, :], vt0[:, pv, k, step * GP:(step + 1) * GP],
                                      start=(k == 0 and s == 0), stop=False)
                    pe.wait_ge(tt_ok, q + 1)
                    if q == 0:
                        pe.wait_ge(gs_first, 16 * 2 * FB * (step + 1))
                    at = q // PER_BATCH * HALF + step * GP
                    pe.matmul(bank, t_t[:, q, :], g_st[:, at:at + GP], start=False, stop=True
                              ).then_inc(tile_done, 1)

            def product_step(bank, slot, c, k):
                half, col = c * TILE // HALF, c * TILE % HALF
                for s, (px, pv) in enumerate(((0, 0), (0, 1), (1, 0))):
                    pe.matmul(bank[:], xt[:, slot, px, k, :], vt[half][:, pv, k, col:col + TILE],
                              start=(k == 0 and s == 0), stop=False)

            def stack_product(bank, slot, c):
                pe.matmul(bank[:], t_t[:, slot, :], g_st[:, c * TILE:(c + 1) * TILE],
                          start=False, stop=True).then_inc(tile_done, 1)

            def batch(ph, it, last=False):
                n = ph.n0 + it * ph.tiles
                q0, g0 = ph.q0 + it * PER_BATCH, ph.g0 + it * ph.groups
                for j in range(PER_BATCH):
                    slot = j % 2
                    if j == 0:
                        pe.wait_ge(bt_in, 16 * (ph.s0 + it + 1))
                    t_product(q0 + j, xt[:, slot], g0 + sum(ph.per_block(i) for i in range(j)))
                    for ci, c in enumerate(ph.chunks):
                        t = j * ph.c + ci
                        jobs = {k: (kind, m, g) for k, kind, m, g in ph.jobs(j, ci)}
                        bank = acc[t % ACC_BANKS]
                        pe.wait_ge(acc_free, n + t + 1)
                        for k in range(KB):
                            if k in jobs and not (last and j == PER_BATCH - 1):
                                kind, m, g = jobs[k]
                                if kind == "x" and m == 0:
                                    pe.wait_ge(x_scaled, q0 + j + 2)
                                if kind == "v" and m == 0:
                                    pe.wait_ge(v_scaled, ROWS + it * 2 + j // 2 + 1)
                                group(g0 + g, g % TR_BANKS, x_nat if kind == "x" else v_nat, m)
                            if ci == 0 and k == KB // 2:
                                tt_turn(q0 + j)
                            product_step(bank, slot, c, k)
                        if ph.rows and j % 2 == 1 and ci == 1:
                            v_spread(ROWS + it * 2 + j // 2, STEPS)
                        if ci == 0:
                            pe.wait_ge(tt_ok, q0 + j + 1)
                        if j == 0:
                            pe.wait_ge(gs_in[c], 32 * (ph.l0[c] + it + 1))
                        stack_product(bank, slot, c)

            def batch_again(ph, it):
                n = ph.n0 + it * ph.tiles
                for j in range(PER_BATCH):
                    slot = j % 2
                    pe.wait_ge(back_in[slot], 32 * (it * (PER_BATCH // 2) + j // 2 + 1))
                    for ci, c in enumerate(ph.chunks):
                        t = j * ph.c + ci
                        bank = acc[t % ACC_BANKS]
                        pe.wait_ge(acc_free, n + t + 1)
                        for k in range(KB):
                            product_step(bank, slot, c, k)
                        if j == 0:
                            pe.wait_ge(gs_in[c], 32 * (ph.l0[c] + it + 1))
                        stack_product(bank, slot, c)

            with pe.Fori(0, p2.batches) as it:
                batch(p2, it)
            pe.wait_ge(a_back, 16)
            for c in range(HALF // TILE):
                g_product(a_again, vt1[:, :, :, c * TILE:(c + 1) * TILE], TILE, STEPS + 2 * c, 2 * ROWS, p3.g0)
            for it in range(p3.batches):
                batch(p3, it, it == p3.batches - 1)
            with pe.Fori(0, p4.batches) as it:
                batch_again(p4, it)


def kernel(x, itok_B_4_50, condB_scale, itok_Bx4096x4096_0_255, condB_wscale, itok_Bx4096_0_255,
           condB_bscale, _lenS, L0_cond_A, L0_cond_B, L1_cond_weight, L1_cond_bias):
    import numpy as np
    from concourse import bacc, mybir
    from concourse.bass_utils import run_bass_kernel_spmd

    nc = bacc.Bacc("TRN2", target_bir_lowering=False, num_devices=1)
    given = {
        "x": x, "ids": itok_B_4_50, "scale": condB_scale, "wq": itok_Bx4096x4096_0_255,
        "wscale": condB_wscale, "bq": itok_Bx4096_0_255, "bscale": condB_bscale, "zp": _lenS,
        "lora_a": L0_cond_A, "lora_b": L0_cond_B, "weight": L1_cond_weight, "bias": L1_cond_bias,
    }
    arrays, aps = {}, {}
    for name, a in given.items():
        a = np.ascontiguousarray(a)
        arrays[f"in_{name}"] = a
        aps[name] = nc.dram_tensor(f"in_{name}", a.shape, mybir.dt.from_np(a.dtype), kind="ExternalInput").ap()
    aps["out"] = nc.dram_tensor("out_0", arrays["in_x"].shape, mybir.dt.float32, kind="ExternalOutput").ap()
    build_program(nc, **aps)
    r = run_bass_kernel_spmd(nc, [arrays], core_ids=[0])
    return r.results[0]["out_0"]
```

```python
def build_program(nc, x, ids, scale, wq, wscale, bq, bscale, zp, lora_a, lora_b, weight, bias, out):
    import concourse.bass as bass
    from concourse import mybir
    from contextlib import ExitStack

    F32, F32R, F16 = mybir.dt.float32, mybir.dt.float32r, mybir.dt.float16
    BF16, I32 = mybir.dt.bfloat16, mybir.dt.int32
    ALU, ACT, AX = mybir.AluOpType, mybir.ActivationFunctionType, mybir.AxisListType

    P = 128
    BATCHES, SEQ, D = x.shape
    OUTS = weight.shape[0]
    ADAPTERS = wq.shape[0]
    RANK = lora_a.shape[2]
    KB = D // P
    BLOCKS = BATCHES * SEQ // P
    PER_BATCH = SEQ // P
    HALF = OUTS // 2
    TILE = 512
    ROWS = HALF // P
    PIECE = 1024
    PIECES = D // PIECE * ADAPTERS
    WQ_SLOTS = 4
    GROUP = 4
    GROUPS = KB // GROUP
    TR_BANKS, ACC_BANKS = 4, 2
    GP = 256
    FIRST = 8
    STEPS = HALF // GP
    STACK = 4 * RANK + 2
    EXP_MASK = 0x7F800000
    SCALE_BITS, INV_BITS = float((2 * 127 + 14) << 23), float((2 * 127) << 23)
    MAX_BITS, MIN_BITS = float(253 << 23), float(1 << 23)

    x_v = x.rearrange("b (t p) i -> (b t) p i", p=P)
    out_v = out.rearrange("b (t p) o -> (b t) p o", p=P)
    w_v = weight.rearrange("(r p) i -> r p i", p=P)
    wq_v = wq.rearrange("a (r p) i -> a r p i", p=P)
    a_v = lora_a.rearrange("n (k p) r -> n p k r", p=P)

    g_dram = nc.dram_tensor("g_stack", (BATCHES, 4 * RANK, OUTS), F32).ap()
    gb_dram = nc.dram_tensor("bias_stack", (2, OUTS), F32).ap()
    KEPT = 3 * BLOCKS // 4
    xt_dram = nc.dram_tensor("xt_parts", (KEPT, P, 2 * KB * P), F16).ap()
    tt_dram = nc.dram_tensor("t_stack", (KEPT, STACK, P), F32).ap()
    bt_dram = nc.dram_tensor("b_parts", (BATCHES, P, KB * 2 * RANK), F16).ap()
    a_dram = nc.dram_tensor("a_parts", (P, 2 * KB * P), F16).ap()

    ctx = ExitStack()
    with ctx:
        def sb(name, shape, dt):
            return ctx.enter_context(nc.sbuf_tensor(name, shape, dt))

        def sem(name):
            return ctx.enter_context(nc.semaphore(name))

        vt0 = sb("vt0", [P, 2, KB, HALF], F16)
        half1 = sb("half1", [P, 2 * KB * HALF], F16)
        vt1 = half1[:].rearrange("p (s k o) -> p s k o", s=2, k=KB)
        vt = [vt0, vt1]
        space = half1[:].bitcast(F32)
        a_nat = space[:, 0:D].rearrange("p (k c) -> p k c", k=KB)
        a_abs = space[:, D:2 * D].rearrange("p (k c) -> p k c", k=KB)
        b_nat = space[:, 2 * D:3 * D]
        bt_all = half1[:, 6 * D:8 * D].rearrange("p (b k c) -> p b k c", b=BATCHES, k=KB)
        x_nat = sb("x_nat", [P, D], F32)
        xt = sb("xt", [P, 2, 2, KB, P], F16)
        xt_more = half1[:, 0:12 * D].rearrange("p (b s k c) -> p b s k c", b=6, s=2, k=KB)
        xt_first = [xt[:, 0], xt[:, 1]] + [xt_more[:, i] for i in (4, 5, 3, 2, 1, 0)]
        x_places = [x_nat[:], space[:, 5 * D:6 * D], x_nat[:], space[:, 0:D]]
        x_places += [x_nat[:], space[:, 0:D], x_nat[:], x_nat[:], x_nat[:]]
        X_OTHER = (1, 3, 5)
        v_other = space[:, 6 * D:7 * D]
        a_first = half1[:, 14 * D:16 * D].rearrange("p (s k c) -> p s k c", s=2, k=KB)
        wq_sb = sb("wq_sb", [P, WQ_SLOTS, PIECE], I32)
        a_again = wq_sb[:].rearrange("p s c -> p (s c)").bitcast(F16)[:, 0:2 * D].rearrange(
            "p (s k c) -> p s k c", s=2, k=KB)
        v_nat = sb("v_nat", [P, D], F32)
        g_half = v_nat[:, 0:HALF]
        g_half_parts = wq_sb[:].rearrange("p s c -> p (s c)").bitcast(F32R)[:, 2 * HALF:4 * HALF]
        junk = sb("junk", [P, PIECE], BF16)
        g_f = sb("g_f", [P, GP], F32)
        g_hi = sb("g_hi", [P, GP], F32R)
        g_lo = sb("g_lo", [P, GP], F32R)
        g_st = sb("g_st", [STACK, OUTS], F32R)
        v_inv = sb("v_inv", [P, OUTS], BF16)
        out_sb = sb("out_sb", [P, 2, TILE], F32)
        bt = sb("bt", [P, KB, 2 * RANK], F16)
        ident = sb("ident", [P, P], F32)
        ones = sb("ones", [P, P], F32)
        diag = sb("diag", [P, P], F32)
        t_lo = sb("t_lo", [P, RANK], F32)
        t_f = sb("t_f", [P, RANK], F32)
        t_st = sb("t_st", [P, STACK], F32R)
        t_t = sb("t_t", [STACK, FIRST, P], F32R)
        b_pair = sb("b_pair", [P, 2], F32R)
        b_row = sb("b_row", [2, P], F32R)
        ids_sb = sb("ids_sb", [1, BATCHES], I32)
        small = sb("small", [P, 4, ADAPTERS], F32)
        zp_i = sb("zp_i", [P, ADAPTERS], I32)
        bq_i = sb("bq_i", [P, P], I32)
        bq_f = sb("bq_f", [P, P], F32)
        bias_rows = sb("bias_rows", [OUTS // P, P], F32)
        coef = sb("coef", [P, 2, ADAPTERS], F32)
        zprod = sb("zprod", [P, ADAPTERS], F32)
        c0 = sb("c0", [P, 1], F32)
        b_col = sb("b_col", [P, OUTS // P], F32)
        sums = sb("sums", [P, 8], F32)
        tot = sb("tot", [P, 1], F32)
        bits = sb("bits", [P, 1], F32)
        x_sc = sb("x_sc", [P, FIRST, 2], F32)
        x_inv = sb("x_inv", [P, KEPT], F32)
        v_sc = sb("v_sc", [P, 3], F32)
        a_sc = sb("a_sc", [P, 2], F32)
        b_sc = sb("b_sc", [P, 2], F32)
        b_tmp = sb("b_tmp", [P, 1], F32)

        acc = [ctx.enter_context(nc.psum_tensor(f"acc{i}", [P, TILE], F32)) for i in range(ACC_BANKS)]
        tr = [ctx.enter_context(nc.psum_tensor(f"tr{i}", [P, TILE], F32)) for i in range(TR_BANKS)]
        g_ps = ctx.enter_context(nc.psum_tensor("g_ps", [P, TILE], F32))
        misc = ctx.enter_context(nc.psum_tensor("misc", [P, TILE], F32))
        t_ps = misc[:, 0:2 * RANK]
        tt_ps = misc[0:STACK, 32:160]
        asum_ps = misc[:, 416:417]
        inv_ps, brow_ps = g_ps[:, 0:128], g_ps[0:2, 128:256]
        bq_ps, bias_ps, abc_ps = g_ps[:, 0:128], g_ps[:, 128:144], g_ps[:, 256:384]

        ids_in, small_in, a_in, b_in, w_in = map(sem, ("ids_in", "small_in", "a_in", "b_in", "w_in"))
        x_in, x_in_other = map(sem, ("x_in", "x_in_other"))
        wq_in = [sem(f"wq_in{s}") for s in range(WQ_SLOTS)]
        ident_ok, bq_ok, bqt_ok = map(sem, ("ident_ok", "bq_ok", "bqt_ok"))
        b_abs, b_scale, b_scaled = map(sem, ("b_abs", "b_scale", "b_scaled"))
        a_absd, a_sum, a_diag, a_bc, a_scaled, a_hi, a_lo = map(
            sem, ("a_absd", "a_sum", "a_diag", "a_bc", "a_scaled", "a_hi", "a_lo"))
        bt_out, bt_in, a_out, a_back = map(sem, ("bt_out", "bt_in", "a_out", "a_back"))
        wq_used, v_sum, v_abs, v_scale, v_scaled, v_diag, v_bc, v_row, gb_out = map(
            sem, ("wq_used", "v_sum", "v_abs", "v_scale", "v_scaled", "v_diag", "v_bc", "v_row", "gb_out"))
        x_abs, x_scale, x_scaled = map(sem, ("x_abs", "x_scale", "x_scaled"))
        tr_done, hi_done, tr_free = map(sem, ("tr_done", "hi_done", "tr_free"))
        t_done, t_split, tt_done, tt_ok = map(sem, ("t_done", "t_split", "tt_done", "tt_ok"))
        g_done, g_free, g_ok, g_out = map(sem, ("g_done", "g_free", "g_ok", "g_out"))
        gs_first = sem("gs_first")
        gs_in = [sem(f"gs_in{c}") for c in range(OUTS // TILE)]
        tile_done, acc_free, out_ready = map(sem, ("tile_done", "acc_free", "out_ready"))
        first_kept = sem("first_kept")
        kept = [sem("kept0"), sem("kept1")]
        back_in = [sem("back_in0"), sem("back_in1")]
        out_free = [sem("out_free0"), sem("out_free1")]

        SETUP_GROUPS = GROUPS * (1 + FIRST + 1 + ROWS)
        NB = BATCHES // 2

        X_FIRST_AT, X_EVERY = 9, 8
        X_LAST_AT = 152
        TILE_FIRST_AT, TILE_EVERY = 49, 4
        B_STEPS = ((2, "b_abs"), (3.5, "b_scale"), (4, "b_turn"), (8, "b_lo"), (8.5, "b_out"))
        A_STEPS = ((9.5, "a_abs"), (10, "a_sum"), (12.5, "a_scale"), (13, "a_spread"), (14.5, "a_scaled"),
                   (16.5, "a_hi"), (20.5, "a_lo"), (22, "a_out"))
        X_STEPS = ((0, "x_abs"), (2, "x_scale"), (2.5, "x_scaled"), (4.1, "x_turn"), (7.5, "x_lo"))
        T_STEPS = ((7.8, "t"), (9.6, "t_parts"), (10.6, "tt"))
        V_STEPS = ((0.5, "v_abs"), (3, "v_scale"), (3.1, "v_scaled"), (4.2, "v_turn"), (7.5, "v_lo"),
                   (8, "v_spread"), (8.2, "v_rows"))
        G_STEPS = ((8.9, "g"), (14, "g_parts"), (15, "g_store"))
        TILE_STEPS = ((0, "tile"), (5, "evacuate"))
        KEEP_AT, KEEP_EVERY = 130, 2

        first_steps = []

        def place(start, steps, i):
            first_steps.extend((start + at, kind, i) for at, kind in steps)

        place(0, B_STEPS + A_STEPS, 0)
        for r in range(ROWS):
            for n in range(0, PIECES, 2):
                place(r * PIECES + n, ((0, "terms"),), (r, n))
            place((r + 1) * PIECES, V_STEPS, r)
        for q in range(FIRST):
            place(X_FIRST_AT + X_EVERY * q, X_STEPS + T_STEPS, q)
            place(KEEP_AT + KEEP_EVERY * q, ((0, "keep"),), q)
        place(X_LAST_AT, X_STEPS, FIRST)
        for step in range(STEPS):
            place(2 * (step + 1) * PIECES, G_STEPS, step)
        for n in range(STEPS * FIRST):
            place(TILE_FIRST_AT + TILE_EVERY * n, TILE_STEPS, n)
        first_steps = [(kind, i) for _, kind, i in sorted(first_steps, key=lambda s: s[0])]
        first_group, count = {}, 0
        for kind, i in first_steps:
            if kind in ("b_turn", "x_turn", "v_turn"):
                first_group[kind, i] = count
                count += GROUPS
        assert count == SETUP_GROUPS

        class Phase:
            def __init__(self, first, batches, chunks, before, rows):
                self.first, self.batches, self.chunks, self.rows = first, batches, chunks, rows
                self.c = len(chunks)
                if self.c == 2:
                    self.at = {(0, 12): "x", (1, 2): "x", (1, 6): "x", (1, 10): "x"}
                else:
                    self.at = {(1, 4): "x", (1, 12): "x", (2, 4): "x", (2, 12): "x"}
                self.tiles = PER_BATCH * self.c
                self.groups = PER_BATCH * GROUPS + rows * GROUPS
                self.q0, self.n0, self.g0, self.s0, self.l0 = before

            def after(self):
                return (self.q0 + self.batches * PER_BATCH, self.n0 + self.batches * self.tiles,
                        self.g0 + self.batches * self.groups, self.s0 + self.batches,
                        [n + self.batches * (c in self.chunks) for c, n in enumerate(self.l0)])

            def jobs(self, j, ci):
                at = dict(self.at)
                if self.rows and j % 2 == 1:
                    at = {(0, 12): "x", (1, 1): "x", (1, 3): "x", (1, 5): "x", (1, 6): "v", (1, 8): "v",
                          (1, 10): "v", (1, 12): "v"}
                found = []
                per_block = [self.per_block(i) for i in range(j)]
                base = sum(per_block)
                order = sorted(at.items())
                seen = {"x": 0, "v": 0}
                for n, ((c, k), kind) in enumerate(order):
                    if c == ci:
                        found.append((k, kind, seen[kind], base + n))
                    seen[kind] += 1
                return found

            def free_for_row(self, i):
                last = [g for j in range(2 * i) for ci in range(self.c) for _, kind, _, g in self.jobs(j, ci)
                        if kind == "v"]
                if i == 0:
                    return self.free_for_row(2) - self.groups
                return max(last) + 1

            def per_block(self, j):
                return GROUPS * (2 if self.rows and j % 2 == 1 else 1)

        FB = FIRST // PER_BATCH
        p2 = Phase(FB, NB, (0, 1), (FIRST, STEPS * FIRST, SETUP_GROUPS, FB, [0] * len(gs_in)), 2)
        p3 = Phase(FB + NB, BATCHES - FB - NB, (0, 1, 2, 3), p2.after(), 0)
        p4 = Phase(0, FB + NB, (2, 3), p3.after(), 0)
        assert NB * p2.rows == ROWS

        block = ctx.enter_context(nc.Block())

        def group_view(bank):
            return bank[:].rearrange("p (m c) -> p m c", m=GROUP)

        def store_g(eng, piece, cols, parts):
            eng.wait_ge(g_ok, piece + 1)
            for dup in range(2):
                for part, src in enumerate(parts):
                    r0 = (2 * part + dup) * RANK
                    eng.dma_start(g_dram[:, r0:r0 + RANK, cols], src.bitcast(F32)).then_inc(g_out, 16)

        def half_part(part, c):
            return g_half_parts[:, part * HALF + c * TILE:part * HALF + (c + 1) * TILE]

        def first_tile(n):
            return n // FIRST, n % FIRST

        @block.sync
        def _(sp):
            AHEAD = 10

            def load_wq(r, pieces):
                for n in pieces:
                    a, h = n // 2, n % 2
                    if not (isinstance(r, int) and r * PIECES + n < WQ_SLOTS):
                        sp.wait_ge(wq_used, r * PIECES + n - WQ_SLOTS + 1)
                    sp.dma_start(wq_sb[:, n % WQ_SLOTS, :],
                                 wq_v[a, bass.ds(r, 1), :, h * PIECE:(h + 1) * PIECE].rearrange(
                                     "r p i -> (r p) i")).then_inc(wq_in[n % WQ_SLOTS], 16)

            def load_weight(r, v, free):
                if free is not None:
                    sp.wait_ge(tr_done, free)
                sp.dma_start(v, w_v[bass.ds(r, 1)].rearrange("r p i -> (r p) i")).then_inc(w_in, 16)

            load_weight(0, v_nat[:], None)
            load_wq(0, range(WQ_SLOTS))
            sp.dma_start(ids_sb[:], ids.rearrange("(a b) -> a b", a=1)).then_inc(ids_in, 16)
            sp.wait_ge(ids_in, 16)
            for b in range(BATCHES):
                n = sp.value_load(ids_sb[0:1, b:b + 1], min_val=0, max_val=lora_a.shape[0] - 1)
                sp.dma_start(b_nat[b * RANK:(b + 1) * RANK, :],
                             lora_b[bass.ds(n, 1)].rearrange("n r i -> (n r) i")).then_inc(b_in, 16)
                sp.dma_start(a_nat[:, :, b * RANK:(b + 1) * RANK],
                             a_v[bass.ds(n, 1)].rearrange("n p k r -> (n p) k r")).then_inc(a_in, 16)
            for r in range(ROWS):
                load_wq(r, range(WQ_SLOTS if r == 0 else 0, AHEAD))
                if r < ROWS - 1:
                    load_weight(r + 1, v_nat[:] if r % 2 else v_other,
                                first_group["v_turn", r - 1] + GROUPS if r else None)
                load_wq(r, range(AHEAD, PIECES))
            with sp.Fori(0, p2.batches) as it:
                for i in range(2):
                    r = ROWS + it * 2 + i
                    load_wq(r, range(WQ_SLOTS))
                    load_weight(r, v_nat[:], p2.g0 + it * p2.groups + p2.free_for_row(i))
                    load_wq(r, range(WQ_SLOTS, PIECES))
            sp.wait_ge(wq_used, 2 * ROWS * PIECES)
            sp.dma_start(wq_sb[:].rearrange("p s c -> p (s c)").bitcast(F16)[:, 0:2 * D],
                         a_dram).then_inc(a_back, 16)
            for c in range(HALF // TILE):
                store_g(sp, STEPS + c, slice(HALF + c * TILE, HALF + (c + 1) * TILE),
                        (half_part(0, c), half_part(1, c)))
            sp.wait_ge(g_out, 16 * 4 * (STEPS + HALF // TILE))
            for slot in range(2):
                sp.wait_ge(kept[slot], 32 * (1 + p2.batches * PER_BATCH // 2))
            with sp.Fori(0, p4.batches) as it:
                for j in range(PER_BATCH):
                    sp.wait_ge(tile_done, p4.n0 + it * p4.tiles + (j - 1) * p4.c + 1)
                    blk = bass.ds((it + p4.first) * PER_BATCH + j, 1)
                    sp.dma_start(xt[:, j % 2].rearrange("p s k c -> p (s k c)"),
                                 xt_dram[blk].rearrange("b p c -> (b p) c")).then_inc(back_in[j % 2], 16)
                    sp.dma_start(t_t[:, j % 2, :].bitcast(F32),
                                 tt_dram[blk].rearrange("b p c -> (b p) c")).then_inc(back_in[j % 2], 16)

        @block.gpsimd
        def _(pool):
            pool.memset(ones[:], 1.0).then_inc(tile_done, 1)
            pool.memset(ident[:], 0.0).then_inc(ident_ok, 1)
            pool.wait_ge(ident_ok, 1)
            pool.affine_select(out=ident[:], in_=ident[:], compare_op=ALU.not_equal, fill=1.0, base=0,
                               pattern=[[-1, P]], channel_multiplier=1).then_inc(ident_ok, 1)

            bt_flat = bt[:].rearrange("p k c -> p (k c)")

            def load_bt(b):
                pool.dma_start(bt_flat, bt_dram[bass.ds(b, 1)].rearrange("b p c -> (b p) c")).then_inc(bt_in, 16)

            pool.wait_ge(bt_out, 16)
            load_bt(0)
            pool.wait_ge(t_done, PER_BATCH)
            load_bt(1)

            def load_first_stacks(step):
                cols = slice(step * GP, (step + 1) * GP)
                pool.wait_ge(g_out, 16 * 4 * (step + 1))
                pool.wait_ge(gb_out, 16 * 2 * (step + 1))
                for b in range(FB):
                    to = slice(b * HALF + step * GP, b * HALF + (step + 1) * GP)
                    pool.dma_start(g_st[0:4 * RANK, to].bitcast(F32), g_dram[b, :, cols]).then_inc(gs_first, 16)
                    pool.dma_start(g_st[4 * RANK:STACK, to].bitcast(F32), gb_dram[:, cols]).then_inc(gs_first, 16)

            def store_tile(dst, n, parity, cols):
                own = out_sb[:, parity, 0:cols.stop - cols.start]
                pool.wait_ge(acc_free, n + ACC_BANKS + 1)
                pool.tensor_tensor(own, own, v_inv[:, cols], ALU.mult).then_inc(out_ready, 1)
                pool.wait_ge(out_ready, n + 1)
                pool.dma_start(dst, own).then_inc(out_free[parity], 16)

            load_first_stacks(0)
            for n in range(STEPS * FIRST):
                step, q = first_tile(n)
                if n == PER_BATCH:
                    pool.wait_ge(t_done, 2 * PER_BATCH)
                    load_bt(2)
                if q == FIRST - 2 and step < STEPS - 1:
                    load_first_stacks(step + 1)
                cols = slice(step * GP, (step + 1) * GP)
                store_tile(out_v[q, :, cols], n, n % 2, cols)

            def stacks_ready(ph):
                pool.wait_ge(g_out, 16 * 4 * (STEPS if ph is p2 else STEPS + HALF // TILE))
                pool.wait_ge(gb_out, 16 * (ph.chunks[-1] + 1) * TILE // P)

            def batch(ph, it, more):
                b = it + ph.first
                n = ph.n0 + it * ph.tiles
                pool.wait_ge(tile_done, n + 1)
                for c in ph.chunks:
                    cols = slice(c * TILE, (c + 1) * TILE)
                    pool.dma_start(g_st[0:4 * RANK, cols].bitcast(F32),
                                   g_dram[bass.ds(b, 1), :, cols].rearrange("b r o -> (b r) o")
                                   ).then_inc(gs_in[c], 16)
                    pool.dma_start(g_st[4 * RANK:STACK, cols].bitcast(F32), gb_dram[:, cols]
                                   ).then_inc(gs_in[c], 16)
                for j in range(PER_BATCH):
                    for ci, c in enumerate(ph.chunks):
                        t = j * ph.c + ci
                        cols = slice(c * TILE, (c + 1) * TILE)
                        store_tile(out_v[bass.ds(b * PER_BATCH + j, 1), :, cols].rearrange("t p o -> (t p) o"),
                                   n + t, t % 2, cols)
                        if j == PER_BATCH - 1 and ci == 0 and more:
                            pool.wait_ge(t_done, ph.q0 + it * PER_BATCH + PER_BATCH)
                            load_bt(b + 1)

            stacks_ready(p2)
            with pool.Fori(0, p2.batches) as it:
                batch(p2, it, True)
            stacks_ready(p3)
            for it in range(p3.batches):
                batch(p3, it, it < p3.batches - 1)
            with pool.Fori(0, p4.batches) as it:
                batch(p4, it, False)
            last = p4.after()[1]
            for s in range(2):
                pool.wait_ge(out_free[s], 16 * (last // 2))

        @block.scalar
        def _(act):
            def load_x(blk):
                act.dma_start(x_nat[:], x_v[bass.ds(blk, 1)].rearrange("t p i -> (t p) i")).then_inc(x_in, 16)

            def load_first_x(q):
                done = x_in_other if q in X_OTHER else x_in
                act.dma_start(x_places[q], x_v[q]).then_inc(done, 16)

            def abs_sums(src, col, done):
                for h in range(2):
                    if h:
                        act.drain()
                    s = act.activation(junk[:], src[:, h * PIECE:(h + 1) * PIECE], ACT.Abs,
                                       bias=c0[:] if done is v_abs else 0.0,
                                       accum_out=sums[:, col + h:col + h + 1])
                s.then_inc(done, 1)

            def hi(g, bank, dst):
                act.wait_ge(tr_done, g + 1)
                act.activation(dst, group_view(tr[bank]), ACT.Copy).then_inc(hi_done, 1)

            def v_abs_sums(r, v):
                act.drain()
                act.wait_ge(v_sum, r + 1)
                abs_sums(v, 2, v_abs)

            def v_to_scale(r, v):
                act.wait_ge(v_scale, r + 1)
                act.activation(v, v, ACT.Identity, bias=v_sc[:, 2:3],
                               scale=v_sc[:, 0:1]).then_inc(v_scaled, 1)

            def v_hi(half, r, m, g, bank):
                o = (r - half * ROWS) * P
                hi(g, bank, vt[half][:, 0, m * GROUP:(m + 1) * GROUP, bass.ds(o, P)])

            def v_rows(r, first=False):
                act.wait_ge(v_bc, r + 1)
                act.activation(v_inv[:, bass.ds(r * P, P)], inv_ps, ACT.Copy)
                if not first:
                    act.wait_ge(gb_out, 16 * r)
                act.activation(b_row[:], brow_ps, ACT.Copy).then_inc(v_row, 1)
                act.wait_ge(v_row, r + 1)
                act.dma_start(gb_dram[:, bass.ds(r * P, P)], b_row[:].bitcast(F32)).then_inc(gb_out, 16)

            def x_abs_sums(q, place=x_nat[:]):
                act.drain()
                if isinstance(q, int) and q in X_OTHER:
                    act.wait_ge(x_in_other, 16 * (X_OTHER.index(q) + 1))
                elif isinstance(q, int) and q < FIRST:
                    act.wait_ge(x_in, 16 * (q + 1 - sum(other < q for other in X_OTHER)))
                else:
                    act.wait_ge(x_in, 16 * (q + 1 - len(X_OTHER)))
                abs_sums(place, 0, x_abs)

            def x_to_scale(q, scale_slot, place=x_nat[:]):
                act.wait_ge(x_scale, q + 1)
                act.activation(place, place, ACT.Copy, scale=x_sc[:, scale_slot, 0:1]).then_inc(x_scaled, 1)

            def x_hi(dst, m, g, bank):
                hi(g, bank, dst[:, 0, m * GROUP:(m + 1) * GROUP, :])

            def tt_copy(q, slot):
                act.wait_ge(tt_done, q + 1)
                act.activation(t_t[:, slot, :], tt_ps, ACT.Copy).then_inc(tt_ok, 1)

            def keep(blk, x_t, slot, done):
                act.dma_start(xt_dram[blk].rearrange("b p c -> (b p) c"),
                              x_t.rearrange("p s k c -> p (s k c)")).then_inc(done, 16)
                act.dma_start(tt_dram[blk].rearrange("b p c -> (b p) c"),
                              t_t[:, slot, :].bitcast(F32)).then_inc(done, 16)

            def evacuate(n, pair, parity, slot, size):
                act.wait_ge(tile_done, n + 2)
                if not (isinstance(pair, int) and pair == 0):
                    act.wait_ge(out_free[parity], 16 * pair)
                act.activation(out_sb[:, parity, 0:size], acc[parity][:, 0:size], ACT.Copy,
                               scale=x_sc[:, slot, 1:2]).then_inc(acc_free, 1)

            for i, src in enumerate((scale, wscale, bscale)):
                act.dma_start(small[:, i, :], src.rearrange("(o a) -> o a", o=1).to_broadcast([P, ADAPTERS])
                              ).then_inc(small_in, 16)
            act.dma_start(zp_i[:], zp.rearrange("(o a) -> o a", o=1).to_broadcast([P, ADAPTERS])).then_inc(small_in, 16)
            act.dma_start(bq_i[:], bq.rearrange("a (r p) -> (a r) p", p=P)).then_inc(small_in, 16)
            act.dma_start(bias_rows[:], bias.rearrange("(r p) -> r p", p=P)).then_inc(small_in, 16)
            load_first_x(0)
            load_first_x(1)

            for kind, i in first_steps:
                g = first_group.get((kind, i))
                if kind == "b_abs":
                    act.wait_ge(b_in, 16 * BATCHES)
                    abs_sums(b_nat, 4, b_abs)
                elif kind == "b_turn":
                    act.wait_ge(b_scale, 1)
                    act.activation(b_nat, b_nat, ACT.Copy, scale=b_sc[:, 0:1]).then_inc(b_scaled, 1)
                    for m in range(GROUPS):
                        act.wait_ge(tr_done, g + m + 1)
                        act.activation(
                            bt_all[:, :, m * GROUP:(m + 1) * GROUP, RANK:].rearrange("p b k r -> p k b r"),
                            tr[m][:].rearrange("p (k b r) -> p k b r", k=GROUP, b=BATCHES),
                            ACT.Copy).then_inc(hi_done, 1)
                elif kind == "b_out":
                    act.wait_ge(tr_free, TR_BANKS + first_group["b_turn", 0] + GROUPS)
                    act.dma_start(bt_dram.rearrange("b p c -> p b c"),
                                  bt_all.rearrange("p b k c -> p b (k c)")).then_inc(bt_out, 16)
                elif kind == "a_abs":
                    act.wait_ge(a_in, 16 * BATCHES)
                    act.activation(a_abs, a_nat, ACT.Abs).then_inc(a_absd, 1)
                elif kind == "a_hi":
                    act.wait_ge(a_scaled, 1)
                    act.activation(a_first[:, 0], a_nat, ACT.Copy).then_inc(a_hi, 1)
                elif kind == "a_out":
                    act.wait_ge(a_hi, 1)
                    act.wait_ge(a_lo, 1)
                    act.dma_start(a_dram, half1[:, 14 * D:16 * D]).then_inc(a_out, 16)
                elif kind == "x_abs":
                    x_abs_sums(i, x_places[i])
                elif kind == "x_scaled":
                    x_to_scale(i, i % FIRST, x_places[i])
                elif kind == "x_turn":
                    if i == 4:
                        act.wait_ge(bt_out, 16)
                    if i == FIRST:
                        act.wait_ge(kept[0], 32)
                    for m in range(GROUPS):
                        x_hi(xt_first[i % FIRST], m, g + m, (g + m) % TR_BANKS)
                    if i + 2 < FIRST - 1:
                        if i + 2 == X_OTHER[1]:
                            act.wait_ge(a_lo, 1)
                        load_first_x(i + 2)
                    elif i >= FIRST - 2:
                        load_x(i + 1)
                elif kind == "tt":
                    tt_copy(i, i)
                elif kind == "v_abs":
                    v_abs_sums(i, v_other if i % 2 else v_nat[:])
                elif kind == "v_scaled":
                    v_to_scale(i, v_other if i % 2 else v_nat[:])
                elif kind == "v_turn":
                    for m in range(GROUPS):
                        v_hi(0, i, m, g + m, (g + m) % TR_BANKS)
                elif kind == "v_rows":
                    v_rows(i, i == 0)
                elif kind == "g_store":
                    store_g(act, i, slice(i * GP, (i + 1) * GP), (g_hi[:], g_lo[:]))
                elif kind == "evacuate":
                    evacuate(i, i // 2, i % 2, i % FIRST, GP)
                elif kind == "keep":
                    act.wait_ge(tt_ok, i + 1)
                    keep(slice(i, i + 1), xt_first[i], i, kept[i] if i < 2 else first_kept)
            act.wait_ge(first_kept, 32 * (FIRST - 2))
            act.wait_ge(a_out, 16)

            def tile_out(ph, it, t):
                evacuate(ph.n0 + it * ph.tiles + t, ph.n0 // 2 + it * (ph.tiles // 2) + t // 2, t % 2,
                         t // ph.c, TILE)

            def batch(ph, it, last=False):
                q0, g0 = ph.q0 + it * PER_BATCH, ph.g0 + it * ph.groups
                for j in range(PER_BATCH):
                    q = q0 + j
                    for ci in range(ph.c):
                        if j or ci:
                            tile_out(ph, it, j * ph.c + ci - 1)
                        more = not (last and j == PER_BATCH - 1)
                        if ci == 0:
                            if more:
                                x_abs_sums(q + 1)
                                x_to_scale(q + 1, (j + 1) % PER_BATCH)
                            if ph is p2:
                                act.wait_ge(kept[j % 2], 32 * (1 + it * 2 + j // 2))
                            tt_copy(q, j % 2)
                            if ph is p2:
                                act.wait_ge(tt_ok, q + 1)
                                keep(bass.ds(q, 1), xt[:, j % 2], j % 2, kept[j % 2])
                        r = ROWS + it * 2 + j // 2
                        if ph.rows and j % 2 == 1 and ci == 0:
                            v_abs_sums(r, v_nat[:])
                            v_to_scale(r, v_nat[:])
                        for k, kind, m, g in ph.jobs(j, ci):
                            if kind == "x" and more:
                                if ph is p2 and m == 0:
                                    act.wait_ge(kept[(j + 1) % 2], 32 * (1 + it * 2 + (j + 1) // 2))
                                x_hi(xt[:, (j + 1) % 2], m, g0 + g, g % TR_BANKS)
                                if m == GROUPS - 1 and not (last and j == PER_BATCH - 2):
                                    load_x(q + 2)
                            elif kind == "v":
                                v_hi(1, r, m, g0 + g, g % TR_BANKS)
                        if ph.rows and j % 2 == 1 and ci == 1:
                            v_rows(r)
                tile_out(ph, it, ph.tiles - 1)

            def batch_again(ph, it):
                act.drain()
                for j in range(PER_BATCH):
                    act.activation(x_sc[:, j, 1:2], x_inv[:, bass.ds((it + ph.first) * PER_BATCH + j, 1)], ACT.Copy)
                act.drain()
                for t in range(ph.tiles):
                    tile_out(ph, it, t)

            with act.Fori(0, p2.batches) as it:
                batch(p2, it)
            for slot in range(2):
                act.wait_ge(kept[slot], 32 * (1 + p2.batches * PER_BATCH // 2))
            for it in range(p3.batches):
                batch(p3, it, it == p3.batches - 1)
            with act.Fori(0, p4.batches) as it:
                batch_again(p4, it)

        @block.vector
        def _(dve):
            def pow2(total, s, inv):
                ti, bi = total.bitcast(I32), bits[:].bitcast(I32)
                dve.drain()
                dve.tensor_scalar(bi, ti, EXP_MASK, None, ALU.bitwise_and)
                dve.drain()
                dve.tensor_scalar(bi, bi, -1.0, SCALE_BITS, ALU.mult, ALU.add)
                dve.drain()
                dve.tensor_scalar(s.bitcast(I32), bi, MAX_BITS, MIN_BITS, ALU.min, ALU.max)
                dve.drain()
                return dve.tensor_scalar(inv.bitcast(I32), s.bitcast(I32), -1.0, INV_BITS, ALU.mult, ALU.add)

            def lo(g, bank, dst, part_hi):
                dve.wait_ge(hi_done, g + 1)
                dve.tensor_tensor(dst, group_view(tr[bank]), part_hi, ALU.subtract).then_inc(tr_free, 1)

            def x_pow2(q, slot):
                dve.wait_ge(x_abs, q + 1)
                dve.tensor_tensor(tot[:], sums[:, 0:1], sums[:, 1:2], ALU.add)
                pow2(tot[:], x_sc[:, slot, 0:1], x_sc[:, slot, 1:2]).then_inc(x_scale, 1)

            def x_lo(dst, m, g, bank):
                ks = slice(m * GROUP, (m + 1) * GROUP)
                lo(g, bank, dst[:, 1, ks, :], dst[:, 0, ks, :])

            def v_terms(r, pieces, v=v_nat[:]):
                for n in pieces:
                    a, h = n // 2, n % 2
                    if n == 0:
                        dve.wait_ge(w_in, 16 * (r + 1))
                    dve.wait_ge(wq_in[n % WQ_SLOTS], 16 * (r * (PIECES // WQ_SLOTS) + n // WQ_SLOTS + 1))
                    if n >= 2:
                        dve.wait_ge(wq_used, r * PIECES + n - 1)
                    dst = v[:, h * PIECE:(h + 1) * PIECE]
                    dve.scalar_tensor_tensor(dst, wq_sb[:, n % WQ_SLOTS, :], coef[:, 0, a:a + 1], dst,
                                             ALU.mult, ALU.add).then_inc(wq_used, 1)
                if n == PIECES - 1:
                    dve.wait_ge(wq_used, (r + 1) * PIECES)
                    own = v[:, bass.ds(r * P, P)]
                    dve.tensor_tensor(own, own, ident[:], ALU.add).then_inc(v_sum, 1)

            def v_pow2(r):
                dve.wait_ge(v_abs, r + 1)
                dve.tensor_tensor(tot[:], sums[:, 2:3], sums[:, 3:4], ALU.add)
                pow2(tot[:], v_sc[:, 0:1], v_sc[:, 1:2])
                dve.drain()
                dve.tensor_scalar(v_sc[:, 2:3], c0[:], v_sc[:, 0:1], None, ALU.mult).then_inc(v_scale, 1)
                dve.tensor_scalar(diag[:], ident[:], v_sc[:, 1:2], None, ALU.mult)
                dve.tensor_scalar(b_tmp[:], b_col[:, bass.ds(r, 1)], v_sc[:, 0:1], None, ALU.mult)
                dve.drain()
                dve.tensor_copy(b_pair[:, 0:1], b_tmp[:])
                dve.drain()
                dve.tensor_tensor(b_pair[:, 1:2], b_tmp[:], b_pair[:, 0:1].bitcast(F32),
                                  ALU.subtract).then_inc(v_diag, 1)

            def v_lo(half, r, m, g, bank):
                o = (r - half * ROWS) * P
                ks = slice(m * GROUP, (m + 1) * GROUP)
                lo(g, bank, vt[half][:, 1, ks, bass.ds(o, P)], vt[half][:, 0, ks, bass.ds(o, P)])

            def t_parts(q, slot):
                dve.wait_ge(t_done, q + 1)
                dve.tensor_copy(t_lo[:], t_ps[:, 0:RANK])
                dve.drain()
                dve.tensor_tensor(t_f[:], t_ps[:, RANK:2 * RANK], t_lo[:], ALU.add)
                dve.drain()
                parts = t_st[:, 0:4 * RANK].rearrange("p (u s r) -> p u s r", u=2, s=2)
                twice = t_f[:].rearrange("p (u r) -> p u r", u=1).to_broadcast([P, 2, RANK])
                dve.tensor_copy(parts[:, :, 0, :], twice)
                dve.tensor_copy(t_st[:, 4 * RANK:STACK], x_sc[:, slot, 0:1].to_broadcast([P, 2]))
                dve.drain()
                dve.tensor_tensor(parts[:, :, 1, :], twice, parts[:, :, 0, :].bitcast(F32),
                                  ALU.subtract).then_inc(t_split, 1)

            def g_parts(n, bank, whole, hi, lo):
                dve.wait_ge(g_done, n + 1)
                dve.tensor_scalar(whole, bank, a_sc[:, 1:2], b_sc[:, 1:2], ALU.mult, ALU.mult).then_inc(g_free, 1)
                dve.drain()
                dve.tensor_copy(hi, whole)
                dve.drain()
                dve.tensor_tensor(lo, whole, hi.bitcast(F32), ALU.subtract).then_inc(g_ok, 1)

            dve.memset(tot[:], 0.0).then_inc(tr_free, TR_BANKS)
            dve.memset(bits[:], 0.0).then_inc(acc_free, ACC_BANKS)
            dve.wait_ge(small_in, 16 * 6)
            dve.tensor_copy(small[:, 3, :], zp_i[:])
            dve.tensor_copy(bq_f[:], bq_i[:]).then_inc(bq_ok, 1)
            dve.tensor_tensor(coef[:, 0, :], small[:, 0, :], small[:, 1, :], ALU.mult)
            dve.tensor_tensor(coef[:, 1, :], small[:, 0, :], small[:, 2, :], ALU.mult)
            dve.drain()
            dve.tensor_tensor(zprod[:], small[:, 0, :], small[:, 3, :], ALU.mult)
            dve.drain()
            dve.tensor_reduce(c0[:], zprod[:], AX.X, ALU.add)
            dve.drain()
            dve.wait_ge(bqt_ok, 1)
            dve.tensor_scalar(b_col[:], bias_ps, c0[:], None, ALU.add)
            for a in range(ADAPTERS):
                dve.drain()
                dve.scalar_tensor_tensor(b_col[:], bq_ps[:, a * KB:(a + 1) * KB], coef[:, 1, a:a + 1], b_col[:],
                                         ALU.mult, ALU.add)
            dve.drain()

            for kind, i in first_steps:
                g = first_group.get((kind.split("_")[0] + "_turn", i))
                if kind == "b_scale":
                    dve.wait_ge(b_abs, 1)
                    dve.tensor_tensor(tot[:], sums[:, 4:5], sums[:, 5:6], ALU.add)
                    pow2(tot[:], b_sc[:, 0:1], b_sc[:, 1:2]).then_inc(b_scale, 1)
                elif kind == "b_lo":
                    for m in range(GROUPS):
                        ks = slice(m * GROUP, (m + 1) * GROUP)
                        dve.wait_ge(hi_done, g + m + 1)
                        dve.tensor_tensor(bt_all[:, :, ks, 0:RANK].rearrange("p b k r -> p k b r"),
                                          tr[m][:].rearrange("p (k b r) -> p k b r", k=GROUP, b=BATCHES),
                                          bt_all[:, :, ks, RANK:].rearrange("p b k r -> p k b r"),
                                          ALU.subtract).then_inc(tr_free, 1)
                elif kind == "a_scale":
                    dve.wait_ge(a_sum, 1)
                    dve.tensor_copy(sums[:, 6:7], asum_ps)
                    pow2(sums[:, 6:7], a_sc[:, 0:1], a_sc[:, 1:2])
                    dve.drain()
                    dve.tensor_scalar(diag[:], ident[:], a_sc[:, 0:1], None, ALU.mult).then_inc(a_diag, 1)
                elif kind == "a_scaled":
                    dve.wait_ge(a_bc, 1)
                    spread = abc_ps.rearrange("p (k c) -> p k c", k=1).to_broadcast([P, KB, P])
                    dve.tensor_tensor(a_nat, a_nat, spread, ALU.mult).then_inc(a_scaled, 1)
                elif kind == "a_lo":
                    dve.wait_ge(a_hi, 1)
                    dve.tensor_tensor(a_first[:, 1], a_nat, a_first[:, 0], ALU.subtract).then_inc(a_lo, 1)
                elif kind == "terms":
                    r, n = i
                    v_terms(r, (n, n + 1), v_other if r % 2 else v_nat[:])
                elif kind == "v_scale":
                    v_pow2(i)
                elif kind == "v_lo":
                    for m in range(GROUPS):
                        v_lo(0, i, m, g + m, (g + m) % TR_BANKS)
                elif kind == "x_scale":
                    x_pow2(i, i % FIRST)
                    if i < FIRST:
                        dve.wait_ge(x_scale, i + 1)
                        dve.tensor_copy(x_inv[:, i:i + 1], x_sc[:, i, 1:2])
                elif kind == "x_lo":
                    for m in range(GROUPS):
                        x_lo(xt_first[i % FIRST], m, g + m, (g + m) % TR_BANKS)
                elif kind == "t_parts":
                    t_parts(i, i)
                elif kind == "g_parts":
                    if i:
                        dve.wait_ge(g_out, 16 * 4 * i)
                    g_parts(i, g_ps[:, 0:GP], g_f[:], g_hi[:], g_lo[:])

            X_POW2_AT = 4.2
            SHARES = [[(n, 2.5 * n + 0.5) for n in range(6)],
                      [(n, 2.5 * (n - 6) + 0.5) for n in range(6, 12)],
                      [(12, 0.5), (13, 1.5), (14, 5), (15, 5.5)], []]

            def batch(ph, it, last=False):
                q0, g0 = ph.q0 + it * PER_BATCH, ph.g0 + it * ph.groups
                for j in range(PER_BATCH):
                    more = not (last and j == PER_BATCH - 1)
                    for ci, c in enumerate(ph.chunks):
                        if ci == 0:
                            t_parts(q0 + j, j)
                            if ph is p2:
                                dve.tensor_copy(x_inv[:, bass.ds(q0 + j, 1)], x_sc[:, j, 1:2])
                        r = ROWS + it * 2 + j // 2
                        jobs = [(k, kind, m, g) for k, kind, m, g in ph.jobs(j, ci) if more]
                        if ci == 0 and more:
                            jobs.append((X_POW2_AT, "x_pow2", 0, 0))
                        if ph.rows:
                            share = SHARES[(j % 2) * 2 + ci]
                            jobs += [(n_at, "terms", n, 0) for n, n_at in share]
                            if (j % 2) * 2 + ci == 2:
                                jobs.append((share[-1][1], "v_pow2", PIECES, 0))
                        for k, kind, m, g in sorted(jobs, key=lambda job: job[0]):
                            if kind == "x":
                                x_lo(xt[:, (j + 1) % 2], m, g0 + g, g % TR_BANKS)
                            elif kind == "v":
                                v_lo(1, r, m, g0 + g, g % TR_BANKS)
                            elif kind == "terms":
                                v_terms(r, (m,))
                            elif kind == "x_pow2":
                                x_pow2(q0 + j + 1, (j + 1) % PER_BATCH)
                            else:
                                v_pow2(r)

            with dve.Fori(0, p2.batches) as it:
                batch(p2, it)
            for c in range(HALF // TILE):
                g_parts(STEPS + c, g_ps[:], g_half[:, c * TILE:(c + 1) * TILE], half_part(0, c), half_part(1, c))
            for it in range(p3.batches):
                batch(p3, it, it == p3.batches - 1)

        @block.tensor
        def _(pe):
            def group(g, bank, src, m):
                pe.wait_ge(tr_free, g + 1)
                for i in range(GROUP):
                    k = m * GROUP + i
                    last = pe.transpose(tr[bank][:, i * P:(i + 1) * P], src[:, k * P:(k + 1) * P], ident[:])
                last.then_inc(tr_done, 1)

            def v_spread(r, pieces):
                if pieces:
                    pe.wait_ge(g_free, pieces)
                pe.wait_ge(v_diag, r + 1)
                pe.matmul(inv_ps, ones[:], diag[:], start=True, stop=True)
                pe.transpose(brow_ps, b_pair[:].bitcast(F32), ident[:]).then_inc(v_bc, 1)

            def g_product(a_parts, v, size, done, rows, groups):
                pe.wait_ge(v_row, rows)
                pe.wait_ge(tr_free, TR_BANKS + groups)
                if done:
                    pe.wait_ge(g_free, done)
                for k in range(KB):
                    for s, (pa, pv) in enumerate(((0, 0), (0, 1), (1, 0))):
                        last = pe.matmul(g_ps[:, 0:size], a_parts[:, pa, k, :], v[:, pv, k, :],
                                         start=(k == 0 and s == 0), stop=(k == KB - 1 and s == 2))
                last.then_inc(g_done, 1)

            def t_product(q, x_t, groups):
                pe.wait_ge(tr_free, TR_BANKS + groups)
                if not (isinstance(q, int) and q == 0):
                    pe.wait_ge(tt_ok, q)
                for k in range(KB):
                    pe.matmul(t_ps, x_t[:, 0, k, :], bt[:, k, :], start=(k == 0), stop=False)
                    last = pe.matmul(t_ps[:, RANK:], x_t[:, 1, k, :], bt[:, k, RANK:],
                                     start=False, stop=(k == KB - 1))
                last.then_inc(t_done, 1)

            def tt_turn(q):
                pe.wait_ge(t_split, q + 1)
                pe.transpose(tt_ps, t_st[:].bitcast(F32), ident[:]).then_inc(tt_done, 1)

            pe.wait_ge(ident_ok, 2)
            pe.wait_ge(bq_ok, 1)
            pe.transpose(bq_ps, bq_f[:], ident[:])
            pe.transpose(bias_ps, bias_rows[:], ident[0:OUTS // P, 0:OUTS // P]).then_inc(bqt_ok, 1)

            for kind, i in first_steps:
                g = first_group.get((kind, i))
                if kind == "b_turn":
                    pe.wait_ge(b_scaled, 1)
                    for m in range(GROUPS):
                        group(g + m, (g + m) % TR_BANKS, b_nat, m)
                elif kind == "a_sum":
                    pe.wait_ge(a_absd, 1)
                    for k in range(KB):
                        last = pe.matmul(asum_ps, a_abs[:, k, :], ones[:, 0:1], start=(k == 0), stop=(k == KB - 1))
                    last.then_inc(a_sum, 1)
                elif kind == "a_spread":
                    pe.wait_ge(a_diag, 1)
                    pe.matmul(abc_ps, ones[:], diag[:], start=True, stop=True).then_inc(a_bc, 1)
                elif kind == "x_turn":
                    pe.wait_ge(x_scaled, i + 1)
                    for m in range(GROUPS):
                        group(g + m, (g + m) % TR_BANKS, x_places[i], m)
                elif kind == "t":
                    pe.wait_ge(bt_in, 16 * (i // PER_BATCH + 1))
                    t_product(i, xt_first[i], first_group["x_turn", i] + GROUPS)
                elif kind == "tt":
                    tt_turn(i)
                elif kind == "v_turn":
                    pe.wait_ge(v_scaled, i + 1)
                    for m in range(GROUPS):
                        group(g + m, (g + m) % TR_BANKS, v_other if i % 2 else v_nat, m)
                elif kind == "v_spread":
                    v_spread(i, i // 2)
                elif kind == "g":
                    if i == 0:
                        pe.wait_ge(a_lo, 1)
                    g_product(a_first, vt0[:, :, :, i * GP:(i + 1) * GP], GP, i, 2 * i + 2,
                              first_group["v_turn", 2 * i + 1] + GROUPS)
                elif kind == "tile":
                    step, q = first_tile(i)
                    bank = acc[i % ACC_BANKS][:, 0:GP]
                    pe.wait_ge(acc_free, i + 1)
                    for k in range(KB):
                        for s, (px, pv) in enumerate(((0, 0), (0, 1), (1, 0))):
                            pe.matmul(bank, xt_first[q][:, px, k, :], vt0[:, pv, k, step * GP:(step + 1) * GP],
                                      start=(k == 0 and s == 0), stop=False)
                    for tile in {0: (), 1: (i - 1, i)}.get(q, (i,)):
                        block_q = tile % FIRST
                        if block_q == 0:
                            pe.wait_ge(gs_first, 16 * 2 * FB * (step + 1))
                        pe.wait_ge(tt_ok, block_q + 1)
                        at = block_q // PER_BATCH * HALF + step * GP
                        pe.matmul(acc[tile % ACC_BANKS][:, 0:GP], t_t[:, block_q, :], g_st[:, at:at + GP],
                                  start=False, stop=True).then_inc(tile_done, 1)

            def product_step(bank, slot, c, k):
                half, col = c * TILE // HALF, c * TILE % HALF
                for s, (px, pv) in enumerate(((0, 0), (0, 1), (1, 0))):
                    pe.matmul(bank[:], xt[:, slot, px, k, :], vt[half][:, pv, k, col:col + TILE],
                              start=(k == 0 and s == 0), stop=False)

            def stack_product(bank, slot, c):
                pe.matmul(bank[:], t_t[:, slot, :], g_st[:, c * TILE:(c + 1) * TILE],
                          start=False, stop=True).then_inc(tile_done, 1)

            def batch(ph, it, last=False):
                n = ph.n0 + it * ph.tiles
                q0, g0 = ph.q0 + it * PER_BATCH, ph.g0 + it * ph.groups
                for j in range(PER_BATCH):
                    slot = j % 2
                    if j == 0:
                        pe.wait_ge(bt_in, 16 * (ph.s0 + it + 1))
                    groups = g0 + sum(ph.per_block(i) for i in range(j))
                    after_rows = ph.rows and j in (0, 2) or ph is p3 and j == 0 and it == 0
                    t_product(q0 + j, xt[:, slot], groups - (GROUPS if after_rows else 0))
                    for ci, c in enumerate(ph.chunks):
                        t = j * ph.c + ci
                        jobs = {k: (kind, m, g) for k, kind, m, g in ph.jobs(j, ci)}
                        bank = acc[t % ACC_BANKS]
                        pe.wait_ge(acc_free, n + t + 1)
                        for k in range(KB):
                            if k in jobs and not (last and j == PER_BATCH - 1):
                                kind, m, g = jobs[k]
                                if kind == "x" and m == 0:
                                    pe.wait_ge(x_scaled, q0 + j + 2)
                                if kind == "v" and m == 0:
                                    pe.wait_ge(v_scaled, ROWS + it * 2 + j // 2 + 1)
                                group(g0 + g, g % TR_BANKS, x_nat if kind == "x" else v_nat, m)
                            if ci == 0 and k == KB // 2:
                                tt_turn(q0 + j)
                            product_step(bank, slot, c, k)
                        if ph.rows and j % 2 == 1 and ci == 1:
                            v_spread(ROWS + it * 2 + j // 2, STEPS)
                        if ci == 0:
                            pe.wait_ge(tt_ok, q0 + j + 1)
                        if j == 0:
                            pe.wait_ge(gs_in[c], 32 * (ph.l0[c] + it + 1))
                        stack_product(bank, slot, c)

            def batch_again(ph, it):
                n = ph.n0 + it * ph.tiles
                for j in range(PER_BATCH):
                    slot = j % 2
                    pe.wait_ge(back_in[slot], 32 * (it * (PER_BATCH // 2) + j // 2 + 1))
                    for ci, c in enumerate(ph.chunks):
                        t = j * ph.c + ci
                        bank = acc[t % ACC_BANKS]
                        pe.wait_ge(acc_free, n + t + 1)
                        for k in range(KB):
                            product_step(bank, slot, c, k)
                        if j == 0:
                            pe.wait_ge(gs_in[c], 32 * (ph.l0[c] + it + 1))
                        stack_product(bank, slot, c)

            pe.wait_ge(tr_free, TR_BANKS + p2.g0)
            with pe.Fori(0, p2.batches) as it:
                batch(p2, it)
            pe.wait_ge(a_back, 16)
            for c in range(HALF // TILE):
                g_product(a_again, vt1[:, :, :, c * TILE:(c + 1) * TILE], TILE, STEPS + c, 2 * ROWS, p3.g0)
            for it in range(p3.batches):
                batch(p3, it, it == p3.batches - 1)
            with pe.Fori(0, p4.batches) as it:
                batch_again(p4, it)


def kernel(x, itok_B_4_50, condB_scale, itok_Bx4096x4096_0_255, condB_wscale, itok_Bx4096_0_255,
           condB_bscale, _lenS, L0_cond_A, L0_cond_B, L1_cond_weight, L1_cond_bias):
    import numpy as np
    from concourse import bacc, mybir
    from concourse.bass_utils import run_bass_kernel_spmd

    nc = bacc.Bacc("TRN2", target_bir_lowering=False, num_devices=1)
    given = {
        "x": x, "ids": itok_B_4_50, "scale": condB_scale, "wq": itok_Bx4096x4096_0_255,
        "wscale": condB_wscale, "bq": itok_Bx4096_0_255, "bscale": condB_bscale, "zp": _lenS,
        "lora_a": L0_cond_A, "lora_b": L0_cond_B, "weight": L1_cond_weight, "bias": L1_cond_bias,
    }
    arrays, aps = {}, {}
    for name, a in given.items():
        a = np.ascontiguousarray(a)
        arrays[f"in_{name}"] = a
        aps[name] = nc.dram_tensor(f"in_{name}", a.shape, mybir.dt.from_np(a.dtype), kind="ExternalInput").ap()
    aps["out"] = nc.dram_tensor("out_0", arrays["in_x"].shape, mybir.dt.float32, kind="ExternalOutput").ap()
    build_program(nc, **aps)
    r = run_bass_kernel_spmd(nc, [arrays], core_ids=[0])
    return r.results[0]["out_0"]
```
